# Optimizing a Trainium2 kernel written in Bass

```python
import numpy as np
import jax
import jax.numpy as jnp

def _softmax(x, axis=-1):
    return jax.nn.softmax(x, axis=axis)

def _gelu(x):
    return jax.nn.gelu(x, approximate=True)

def _silu(x):
    return jax.nn.silu(x)

def _sigmoid(x):
    return jax.nn.sigmoid(x)

def _layernorm(x, axis=-1, eps=1e-05):
    m = jnp.mean(x, axis=axis, keepdims=True)
    v = jnp.var(x, axis=axis, keepdims=True)
    return (x - m) / jnp.sqrt(v + eps)

def _scatter_add(tgt, idx, src, axis=0):
    return tgt.at[idx].add(src)

def _segment_sum(src, seg, n):
    return jax.ops.segment_sum(src, seg, n)
kernel_name = 'mk_macaron_d1_jaxref_r8_a50c6d'

def setup_inputs(seed: int=0):
    np.random.seed(seed)
    _w = jnp.asarray

    def _L0_attn_setup():
        import jax, jax.numpy as jnp
        import numpy as np
        B, S, D = (8, 512, 128)
        WIN = 257
        HALF = WIN // 2
        BL = 32

        def _blockify(t, nb):
            b, s, d = t.shape
            tp = jnp.pad(t, ((0, 0), (BL, BL), (0, 0)))
            tb = tp.reshape(b, nb + 2, BL, d)
            return jnp.concatenate([tb[:, :-2], tb[:, 1:-1], tb[:, 2:]], axis=2)

        def _local_attention(q, k, v):
            b, s, d = q.shape
            nb = s // BL
            qb = q.reshape(b, nb, BL, d)
            kb = _blockify(k, nb)
            vb = _blockify(v, nb)
            scale = 1.0 / np.sqrt(d).astype(np.float32)
            scores = jnp.einsum('bnqd,bnkd->bnqk', qb, kb) * scale
            blk = jnp.arange(nb)[:, None, None]
            r = jnp.arange(BL)[None, :, None]
            c = jnp.arange(3 * BL)[None, None, :]
            i = blk * BL + r
            j = (blk - 1) * BL + c
            rel = j - i
            valid = (rel >= -HALF) & (rel <= HALF) & (j >= 0) & (j < s)
            scores = jnp.where(valid[None], scores, -jnp.inf)
            weights = jax.nn.softmax(scores, axis=-1)
            out = jnp.einsum('bnqk,bnkd->bnqd', weights, vb)
            return out.reshape(b, s, d)
        key = jax.random.key(seed)
        ks = jax.random.split(key, 7)
        s = 0.02
        return {'x': jax.random.normal(ks[0], (B, S, D), jnp.float32), 'Wq': jax.random.normal(ks[1], (D, D), jnp.float32) * s, 'bq': jnp.zeros((D,), jnp.float32), 'Wk': jax.random.normal(ks[2], (D, D), jnp.float32) * s, 'bk': jnp.zeros((D,), jnp.float32), 'Wv': jax.random.normal(ks[3], (D, D), jnp.float32) * s, 'bv': jnp.zeros((D,), jnp.float32)}
    _L0_attn_in = _L0_attn_setup()

    def _L0_ffn_setup():
        import jax, jax.numpy as jnp
        import numpy as np
        B, S, D = (1, 256, 128)
        F = 176
        E = 16
        K = 2
        CAP_FACTOR = 1.25

        def _mlp(h, wg, wu, wd):
            return jax.nn.silu(h @ wg) * (h @ wu) @ wd
        key = jax.random.key(seed)
        ks = jax.random.split(key, 10)
        sd = 0.02
        return {'x': jax.random.normal(ks[0], (B, S, D), jnp.float32), 'router_w': jax.random.normal(ks[1], (D, E), jnp.float32) * sd, 'router_b': jnp.zeros((E,), jnp.float32), 'w_gate': jax.random.normal(ks[2], (E, D, F), jnp.float32) * sd, 'w_up': jax.random.normal(ks[3], (E, D, F), jnp.float32) * sd, 'w_down': jax.random.normal(ks[4], (E, F, D), jnp.float32) * sd, 'sw_gate': jax.random.normal(ks[5], (D, F), jnp.float32) * sd, 'sw_up': jax.random.normal(ks[6], (D, F), jnp.float32) * sd, 'sw_down': jax.random.normal(ks[7], (F, D), jnp.float32) * sd}
    _L0_ffn_in = _L0_ffn_setup()
    _d = {'L0_attn_x': _L0_attn_in['x'], 'L0_attn_Wq': _L0_attn_in['Wq'], 'L0_attn_bq': _L0_attn_in['bq'], 'L0_attn_Wk': _L0_attn_in['Wk'], 'L0_attn_bk': _L0_attn_in['bk'], 'L0_attn_Wv': _L0_attn_in['Wv'], 'L0_attn_bv': _L0_attn_in['bv'], 'L0_ffn_router_w': _L0_ffn_in['router_w'], 'L0_ffn_router_b': _L0_ffn_in['router_b'], 'L0_ffn_w_gate': _L0_ffn_in['w_gate'], 'L0_ffn_w_up': _L0_ffn_in['w_up'], 'L0_ffn_w_down': _L0_ffn_in['w_down'], 'L0_ffn_sw_gate': _L0_ffn_in['sw_gate'], 'L0_ffn_sw_up': _L0_ffn_in['sw_up'], 'L0_ffn_sw_down': _L0_ffn_in['sw_down']}
    _x0 = _d['L0_attn_x']
    _d['L0_attn_x'] = jax.random.normal(jax.random.fold_in(jax.random.key(seed), 1), (8, 1024, 128), dtype=_x0.dtype)
    del _x0
    return _d

def reference(L0_attn_x, L0_attn_Wq, L0_attn_bq, L0_attn_Wk, L0_attn_bk, L0_attn_Wv, L0_attn_bv, L0_ffn_router_w, L0_ffn_router_b, L0_ffn_w_gate, L0_ffn_w_up, L0_ffn_w_down, L0_ffn_sw_gate, L0_ffn_sw_up, L0_ffn_sw_down):

    def _L0_attn_ref(x, Wq, bq, Wk, bk, Wv, bv):
        import jax, jax.numpy as jnp
        import numpy as np
        B, S, D = (8, 512, 128)
        WIN = 257
        HALF = WIN // 2
        BL = 32

        def _blockify(t, nb):
            b, s, d = t.shape
            tp = jnp.pad(t, ((0, 0), (BL, BL), (0, 0)))
            tb = tp.reshape(b, nb + 2, BL, d)
            return jnp.concatenate([tb[:, :-2], tb[:, 1:-1], tb[:, 2:]], axis=2)

        def _local_attention(q, k, v):
            b, s, d = q.shape
            nb = s // BL
            qb = q.reshape(b, nb, BL, d)
            kb = _blockify(k, nb)
            vb = _blockify(v, nb)
            scale = 1.0 / np.sqrt(d).astype(np.float32)
            scores = jnp.einsum('bnqd,bnkd->bnqk', qb, kb) * scale
            blk = jnp.arange(nb)[:, None, None]
            r = jnp.arange(BL)[None, :, None]
            c = jnp.arange(3 * BL)[None, None, :]
            i = blk * BL + r
            j = (blk - 1) * BL + c
            rel = j - i
            valid = (rel >= -HALF) & (rel <= HALF) & (j >= 0) & (j < s)
            scores = jnp.where(valid[None], scores, -jnp.inf)
            weights = jax.nn.softmax(scores, axis=-1)
            out = jnp.einsum('bnqk,bnkd->bnqd', weights, vb)
            return out.reshape(b, s, d)
        q = x @ Wq + bq
        k = x @ Wk + bk
        v = x @ Wv + bv
        return _local_attention(q, k, v)

    def _L0_ffn_ref(x, router_w, router_b, w_gate, w_up, w_down, sw_gate, sw_up, sw_down):
        import jax, jax.numpy as jnp
        import numpy as np
        B, S, D = (1, 256, 128)
        F = 176
        E = 16
        K = 2
        CAP_FACTOR = 1.25

        def _mlp(h, wg, wu, wd):
            return jax.nn.silu(h @ wg) * (h @ wu) @ wd
        b, s, d = x.shape
        N = b * s
        NK = N * K
        C = int(np.ceil(CAP_FACTOR * NK / E))
        x_tokens = x.reshape(N, d)
        logits = x_tokens @ router_w + router_b
        probs = jax.nn.softmax(logits, axis=-1)
        vals, idx = jax.lax.top_k(probs, K)
        vals = vals / (jnp.sum(vals, axis=-1, keepdims=True) + 1e-09)
        idx_flat = idx.reshape(NK)
        vals_flat = vals.reshape(NK)
        oh_e = jax.nn.one_hot(idx_flat, E, dtype=x.dtype)
        pos = (jnp.cumsum(oh_e, axis=0) * oh_e).sum(axis=1) - 1
        within = (pos < C).astype(x.dtype)
        pos_c = jnp.clip(pos, 0, C - 1).astype(jnp.int32)
        token_ids = jnp.arange(NK) // K
        x_pair = x_tokens[token_ids] * within[:, None]
        expert_inputs = jnp.zeros((E, C, d), x.dtype).at[idx_flat, pos_c].add(x_pair)
        expert_outputs = jax.vmap(_mlp)(expert_inputs, w_gate, w_up, w_down)
        gathered = expert_outputs[idx_flat, pos_c] * (vals_flat * within)[:, None]
        output_tokens = gathered.reshape(N, K, d).sum(axis=1)
        return x + _mlp(x, sw_gate, sw_up, sw_down) + output_tokens.reshape(b, s, d)
    x = L0_attn_x
    x = x + 0.5 * _L0_ffn_ref(_layernorm(x, axis=-1), L0_ffn_router_w, L0_ffn_router_b, L0_ffn_w_gate, L0_ffn_w_up, L0_ffn_w_down, L0_ffn_sw_gate, L0_ffn_sw_up, L0_ffn_sw_down)
    x = x + _L0_attn_ref(_layernorm(x, axis=-1), L0_attn_Wq, L0_attn_bq, L0_attn_Wk, L0_attn_bk, L0_attn_Wv, L0_attn_bv)
    x = x + 0.5 * _L0_ffn_ref(_layernorm(x, axis=-1), L0_ffn_router_w, L0_ffn_router_b, L0_ffn_w_gate, L0_ffn_w_up, L0_ffn_w_down, L0_ffn_sw_gate, L0_ffn_sw_up, L0_ffn_sw_down)
    return x

_drawn_inputs = setup_inputs


def setup_inputs(seed=0):
    import zlib

    import numpy as np

    out = dict(_drawn_inputs(seed))
    spreads = {'L0_attn_bq': (0.0, 0.8),
     'L0_attn_bk': (0.0, 0.8),
     'L0_attn_bv': (0.0, 0.1),
     'L0_ffn_router_b': (0.0, 0.8)}
    factors = {'L0_attn_Wq': 8.0,
     'L0_attn_Wk': 8.0,
     'L0_attn_Wv': 3.602,
     'L0_ffn_router_w': 8.0,
     'L0_ffn_w_gate': 8.0,
     'L0_ffn_w_up': 8.0,
     'L0_ffn_w_down': 8.0,
     'L0_ffn_sw_gate': 8.0,
     'L0_ffn_sw_up': 8.0,
     'L0_ffn_sw_down': 8.0}
    for name, (base, spread) in spreads.items():
        noise = np.random.default_rng([zlib.crc32(name.encode()), seed]).standard_normal(out[name].shape)
        drawn = base * np.exp(spread * noise) if base else spread * noise
        out[name] = jnp.asarray(drawn.astype(out[name].dtype))
    for name, factor in factors.items():
        out[name] = (out[name] * factor).astype(out[name].dtype)
    return out
```

```python
from contextlib import ExitStack

import concourse.bass as bass
from concourse import mybir

F32 = mybir.dt.float32
F16 = mybir.dt.float16
BF16 = mybir.dt.bfloat16
I32 = mybir.dt.int32
U32 = mybir.dt.uint32
ALU = mybir.AluOpType
ACT = mybir.ActivationFunctionType
AX_X = mybir.AxisListType.X

P = 128
D = 128
E = 16
TOPK = 2
F = 176
FA = 128
FB = F - FA
UB = 64
NTOK = 8 * 1024
CAP = -(-5 * NTOK * TOPK // (4 * E))
NB = 8
TB = 8
BT = TB * P
CH = 256
CB = BT // CH
CE = CAP // CH
JE = CAP // P
NCH = E * CE
SW = D + 2
BW = BT + 2 * TB
GW = 2 * FA + 112
BL = 32
WIN = P + 2 * BL
HW_ = WIN // 2
PADT = BT + 2 * BL
WS = 64.0
BIG = float(1 << 20)
MAGIC = 0x5F3759DF
EPS = 1e-5
ATT = float(1.0 / (D ** 0.5))
LOOPS = False
RING = CE

K_ID, K_TRI, K_ONE, K_BLK = 0, 128, 256, 384
K_MASK = 512
K_IOTA = K_MASK + 3 * WIN
K_T2 = K_IOTA + E
K_POS = K_T2 + TB
K_N = K_POS + JE

R_BASE = [0, NB * CB + NCH]
E_BASE = [NB * CB, 2 * NB * CB + NCH]


def wait(eng, sem, value):
    if isinstance(value, int) and value <= 0:
        return
    eng.wait_ge(sem, value)


def wait_alone(eng, sem, value):
    if isinstance(value, int):
        wait(eng, sem, value)
    else:
        eng.wait_ge(sem, 1)
        eng.wait_ge(sem, value)


def run_steps(eng, pieces, n, unroll):
    last = max(lag for _, lag in pieces)

    def peeled(s):
        for fn, lag in pieces:
            if 0 <= s - lag < n:
                fn(s - lag, (s - lag) % unroll, (s - lag) // unroll)

    if not LOOPS:
        for s in range(n + last):
            peeled(s)
        return
    for s in range(unroll):
        peeled(s)
    with eng.Fori(1, n // unroll) as it:
        for k in range(unroll):
            for fn, lag in pieces:
                fn(it * unroll + (k - lag), (k - lag) % unroll, it + (k - lag) // unroll)
    for s in range(n, n + last):
        peeled(s)


class Chain:

    def __init__(self, eng, sem, per_item, item):
        self.eng, self.sem, self.base, self.n = eng, sem, per_item * item, 0
        self.per_item = per_item

    def add(self, ins):
        self.n += 1
        ins.then_inc(self.sem, 1)
        return self.n

    def after(self, n=None):
        wait(self.eng, self.sem, self.base + (self.n if n is None else n))

    def end(self):
        assert self.n == self.per_item, (self.n, self.per_item)


def build(nc, x, wq, bq, wk, bk, wv, bv, rw, rb, wg, wu, wd, sg, su, sd, consts, out):
    ctx = ExitStack()

    def sb(name, shape, dt=F32):
        return ctx.enter_context(nc.sbuf_tensor(name, shape, dt))

    def ps(name, shape, dt=F32):
        return ctx.enter_context(nc.psum_tensor(name, shape, dt))

    def sem(name):
        return ctx.enter_context(nc.semaphore(name))

    def sems(name, n):
        return [sem(f"{name}{i}") for i in range(n)]

    with ctx:
        slots = nc.dram_tensor("slots", (E * CAP, SW), F32, kind="Internal").ap()
        yrows = nc.dram_tensor("yrows", (TOPK * NTOK, D), F32, kind="Internal").ap()
        saved = [nc.dram_tensor(f"saved{i}", (NB, P, BW), F32, kind="Internal").ap() for i in range(2)]

        cst = sb("cst", [P, K_N])
        zero = sb("zero", [P, 1024])
        idh = sb("idh", [P, P], F16)
        tri = sb("tri", [P, P], BF16)
        one = sb("one", [P, P], BF16)
        blk = sb("blk", [P, P], BF16)
        msk = sb("msk", [P, 3, WIN], BF16)
        bcol = sb("bcol", [P, 2])
        bvr = sb("bvr", [P, D])
        rbr = sb("rbr", [P, E])
        wraw = sb("wraw", [P, 3 * D + E])
        whl = sb("whl", [P, 2, 3 * D + E], F16)
        gst = [sb(f"gst{i}", [P, GW]) for i in range(3)]
        ghl = [sb(f"ghl{i}", [P, 2, GW], F16) for i in range(3)]
        wdn = [sb(f"wdn{i}", [P, 2, D]) for i in range(3)]
        st = [sb(f"st{i}", [P, TB, 6]) for i in "rc"]
        mv = [sb(f"mv{i}", [P, TB, 2]) for i in "rc"]
        ve = [sb(f"ve{i}", [P, TB]) for i in "rc"]
        nt = [sb(f"nt{i}", [P, 2, TB]) for i in "rc"]
        rs = [sb(f"rs{i}", [P, 2, TB]) for i in "rc"]
        nmr = [sb(f"nmr{i}", [P, TB]) for i in "rc"]
        X = [sb(f"X{i}", [P, TB, D]) for i in range(2)]
        xnr = sb("xnr", [P, TB, D])
        stg = [sb(f"stg{i}", [P, TB, SW]) for i in range(2)]
        xtr = sb("xtr", [P, 2, BT], F16)
        base = [sb(f"base{i}", [P, BW]) for i in range(2)]
        lg = sb("lg", [P, TB, E + 1])
        m8 = sb("m8", [P, TB, 8])
        i8 = sb("i8", [P, TB, 8], U32)
        oh = sb("oh", [P, TB, 2, E])
        ohs = sb("ohs", [P, TB, E], BF16)
        ec = sb("ec", [P, TB, 2])
        dl = sb("dl", [P, TB, E + 1])
        ex = sb("ex", [P, TB, E + 1])
        zz = sb("zz", [P, 4, TB])
        pp = sb("pp", [P, TB, 2])
        ww = sb("ww", [P, TB, 2])
        prod = sb("prod", [P, TB, 2, E])
        pk = sb("pk", [P, TB, 2])
        ov = sb("ov", [P, TB, 2])
        s1 = sb("s1", [P, TB, 2])
        slot_i = [sb(f"slot_i{i}", [P, TB, 2], I32) for i in range(2)]
        t2run = sb("t2run", [P, TB])
        mred = sb("mred", [P, E])
        macc = sb("macc", [P, E])
        maccb = sb("maccb", [P, E], BF16)
        cnt = sb("cnt", [P, E])
        sA = [sb(f"sA{i}", [P, CH]) for i in range(2)]
        sB = [sb(f"sB{i}", [P, CH]) for i in range(2)]
        hA = [sb(f"hA{i}", [P, CH]) for i in range(2)]
        hB = [sb(f"hB{i}", [P, CH]) for i in range(2)]
        xe = [sb(f"xe{i}", [P, JE, SW]) for i in range(2)]
        xte = [sb(f"xte{i}", [P, 2, CH], F16) for i in range(2)]
        yst = [sb(f"yst{i}", [P, 2, D]) for i in range(RING)]
        inval = sb("inval", [P, JE])
        t2k = sb("t2k", [P, JE])
        row_i = [sb(f"row_i{i}", [P, JE], I32) for i in range(2)]
        bc = [sb(f"bc{i}", [P, BW]) for i in range(2)]
        yin = [sb(f"yin{i}", [P, TB, 2, D]) for i in range(2)]
        x1 = [sb(f"x1{i}", [P, TB, D]) for i in range(2)]
        x1b = [sb(f"x1b{i}", [P, TB, D]) for i in range(2)]
        xnc = sb("xnc", [P, TB, D])
        hlc = sb("hlc", [P, 2, TB, D], F16)
        xtc = [sb(f"xtc{i}", [P, 2, PADT], F16) for i in range(2)]
        qT = [sb(f"qT{i}", [P, BT]) for i in range(2)]
        kT = [sb(f"kT{i}", [P, PADT]) for i in range(2)]
        mx = [sb(f"mx{i}", [P, 2]) for i in range(2)]
        nm = [sb(f"nm{i}", [P, 2]) for i in range(2)]
        pr = [sb(f"pr{i}", [P, 2, WIN]) for i in range(2)]
        rsum = [sb(f"rsum{i}", [P, 2]) for i in range(2)]
        rinv = [sb(f"rinv{i}", [P, 2]) for i in range(2)]
        pts = [sb(f"pts{i}", [HW_, 2, 2, P]) for i in range(2)]
        vs = [sb(f"vs{i}", [HW_, 2, 2, D]) for i in range(2)]

        psGU = [ps(f"psGU{i}", [P, 2, CH]) for i in range(2)]
        psR_ = [ps(f"psR{i}", [P, 512]) for i in range(2)]
        psT_ = ps("psT", [P, 1024], F16)
        psY_ = ps("psY", [P, 512])
        psS = ps("psS", [P, 512])
        psP = ps("psP", [P, 512])
        psR = [t[:, 0:CH] for t in psR_]
        psV = psR_[0][0:HW_, :].rearrange("p (b d) -> p b d", d=D)
        psO = psR_[1][:, 0:2 * D].rearrange("p (t d) -> p t d", t=2)
        psT = psT_[:, 0:2 * CH].rearrange("p (h c) -> p h c", h=2)
        psL = psY_[:, 0:TB * E]
        psPos = psY_[:, TB * E:2 * TB * E]
        psY = psY_[:, 2 * D:4 * D].rearrange("p (t d) -> p t d", t=2)
        psS2 = psS[:, 0:2 * WIN].rearrange("p (t c) -> p t c", t=2)
        psPT = psP[0:HW_, :].rearrange("p (t w q) -> p t w q", t=2, w=2)
        psTC = [t[:, 0:CH].bitcast(F16).rearrange("p (h c) -> p h c", h=2) for t in (psS, psP)]

        ld_c = sem("const_loaded")
        ld_w = sem("weights_loaded")
        zeroed = sem("zero_tile_ready")
        pads = sem("pads_zeroed")
        split0 = sem("fixed_weights_split")
        fill_s = sem("slots_filled")
        fill_y = sem("yrows_filled")
        x_ld = sems("x_loaded", 2)
        x_dv = sem("x2_done")
        ln_ch = sems("ln_chain", 2)
        ln_ok = sems("ln_stats_done", 2)
        xn_ok = sems("xn_done", 2)
        hi_ok = sems("hi_done", 2)
        lo_ok = sems("lo_done", 2)
        t_ok = sem("transposed")
        xt_ok = sem("xt_copied")
        lg_ok = sem("logits_done")
        rt_ch = sem("route_chain")
        ohs_ok = sem("onehot_done")
        dl_ok = sem("delta_done")
        ex_ok = sem("exp_done")
        pos_ok = sem("positions_done")
        rt2_ch = sem("position_chain")
        idx_ok = sem("slot_index_done")
        cnt_mm = sem("count_summed")
        cnt_ok = sem("count_copied")
        scat = sems("rows_scattered", 2)
        gu_ok = sem("gate_up_done")
        silu_ok = sem("silu_done")
        h_ok = sem("hidden_done")
        y_ok = sem("mlp_out_done")
        y_cp = sem("mlp_out_taken")
        sv = sems("batch_saved", 2)
        xe_ld = sems("slots_loaded", 2)
        we_ld = sems("expert_loaded", 2)
        wsp = sem("expert_split")
        ri_ch = sem("row_chain")
        esp_ch = sem("expert_hi_done")
        sp_ch = sem("fixed_hi_done")
        pad_ch = sem("pads_chain")
        ysc = sems("results_scattered", RING)
        c_ld = sems("combine_loaded", 2)
        cb_ch = sem("combine_chain")
        x1_ok = sem("x1_done")
        x1b_ok = sem("x1_bias_done")
        tc_ok = sem("c_transposed")
        xtc_ok = sem("c_xt_copied")
        qk_ok = sem("qk_done")
        qk_cp = sem("qk_copied")
        v_ok = sem("v_done")
        v_cp = sem("v_copied")
        s_ok = sem("scores_done")
        mx_ok = sem("max_done")
        nm_ok = sem("negmax_done")
        p_ok = sem("probs_done")
        pt_ok = sem("probs_transposed")
        pt_cp = sem("probs_t_copied")
        o_ok = sem("attention_done")
        ri_ok = sem("inverse_sum_done")
        out_ok = sems("out_stored", 2)

        x_v = x.rearrange("b (j p) d -> b p j d", p=P)
        out_v = out.rearrange("b (j p) d -> b p j d", p=P)
        slots_v = slots.rearrange("(e p j) w -> e p (j w)", e=E, p=P)
        yr_v = yrows.rearrange("(m j p k) d -> m p j (k d)", m=NB, j=TB, p=P)

        def hi_of(rows):
            return rows[:, :, 0:D // 2].bitcast(F16)

        def lo_of(rows):
            return rows[:, :, D // 2:D].bitcast(F16)

        block = ctx.enter_context(nc.Block())

        def load_mlp(sp, i, g, u, d, s):
            sp.dma_start(gst[i][:, 0:FA], g[:, 0:FA]).then_inc(s, 16)
            sp.dma_start(gst[i][:, FA:2 * FA], u[:, 0:FA]).then_inc(s, 16)
            sp.dma_start(gst[i][:, 2 * FA:2 * FA + FB], g[:, FA:F]).then_inc(s, 16)
            sp.dma_start(gst[i][:, 2 * FA + UB:2 * FA + UB + FB], u[:, FA:F]).then_inc(s, 16)
            sp.dma_start(wdn[i][:, 0, :], d[0:FA, :]).then_inc(s, 16)
            sp.dma_start(wdn[i][UB:UB + FB, 1, :], d[FA:F, :]).then_inc(s, 16)

        @block.sync
        def _(sp):
            sp.dma_start(cst[:], consts).then_inc(ld_c, 16)
            xi = x_v

            def load_x(r, k, u):
                if isinstance(r, int):
                    wait(sp, lo_ok[0], 2 * (r - 1))
                else:
                    sp.wait_ge(lo_ok[0], r * 2 - 2)
                src = xi[r] if isinstance(r, int) else xi[bass.ds(r, 1)].rearrange("o p j d -> (o p) j d")
                sp.dma_start(X[k][:], src).then_inc(x_ld[k], 16)

            def save(layer):
                def f(r, k, u):
                    g = r + NB * layer
                    wait(sp, y_cp, r * CB + (R_BASE[layer] + CB))
                    wait(sp, rt2_ch, (g + 1) * N_RT2)
                    dst = saved[layer][r] if isinstance(r, int) else \
                        saved[layer][bass.ds(r, 1)].rearrange("o p w -> (o p) w")
                    sp.dma_start(dst, base[k][:]).then_inc(sv[k], 16)
                return f

            load_x(0, 0, 0)
            load_x(1, 1, 0)
            for i, w in enumerate((wq, wk, wv)):
                sp.dma_start(wraw[:, i * D:(i + 1) * D], w).then_inc(ld_w, 16)
            sp.dma_start(wraw[:, 3 * D:3 * D + E], rw).then_inc(ld_w, 16)
            sp.dma_start(bcol[:, 0:1], bq.rearrange("(p o) -> p o", o=1)).then_inc(ld_w, 16)
            sp.dma_start(bcol[:, 1:2], bk.rearrange("(p o) -> p o", o=1)).then_inc(ld_w, 16)
            sp.dma_start(bvr[:], bv.rearrange("(o d) -> o d", o=1).broadcast_to([P, D])).then_inc(ld_w, 16)
            sp.dma_start(rbr[:], rb.rearrange("(o d) -> o d", o=1).broadcast_to([P, E])).then_inc(ld_w, 16)
            sp.wait_ge(pads, 1)
            load_mlp(sp, 2, sg, su, sd, ld_w)
            sp.wait_ge(zeroed, 1)
            words = E * CAP * SW // P
            zw = 1024
            sl = slots.rearrange("(p a) w -> p (a w)", p=P)
            n0 = 0
            while n0 < words:
                n1 = min(words, n0 + 8 * zw)
                full = (n1 - n0) // zw
                if full:
                    sp.dma_start(sl[:, n0:n0 + full * zw].rearrange("p (a w) -> p a w", w=zw),
                                 zero[:, :].rearrange("p (o w) -> p o w", o=1).broadcast_to([P, full, zw])
                                 ).then_inc(fill_s, 16)
                    n0 += full * zw
                else:
                    sp.dma_start(sl[:, n0:n1], zero[:, 0:n1 - n0]).then_inc(fill_s, 16)
                    n0 = n1
            yl = yrows.rearrange("(p a) w -> p (a w)", p=P)
            for i in range(2):
                sp.dma_start(yl[:, i * 8 * zw:(i + 1) * 8 * zw].rearrange("p (a w) -> p a w", w=zw),
                             zero[:, :].rearrange("p (o w) -> p o w", o=1).broadcast_to([P, 8, zw])
                             ).then_inc(fill_y, 16)

            def load_next(r, k, u):
                load_x(r, k, u)

            def sp_r0(r, k, u):
                save(0)(r, k, u)

            for r in range(2):
                load_x(r + 2, r, 1)
                sp_r0(r, r, 0)
            for it in range(1, NB // 2 - 1):
                for k in range(2):
                    load_x(it * 2 + (k + 2), k, it + 1)
                    sp_r0(it * 2 + k, k, it)
            for r in range(NB - 2, NB):
                sp_r0(r, r % 2, r // 2)

            def sp_e(layer):
                for k in range(2):
                    sp.wait_ge(scat[k], 16 * 2 * TB * (NB // 2) * (layer + 1))

                def f(e, k, u):
                    g = e + E * layer
                    wait(sp, t_ok, e * CE + (E_BASE[layer] - CE) if not isinstance(e, int) or e > 1 else 0)
                    wait(sp, ri_ch, (g - 1) * 3)
                    src = slots_v[e] if isinstance(e, int) else slots_v[bass.ds(e, 1)].rearrange("o p w -> (o p) w")
                    sp.dma_start(xe[k][:].rearrange("p j w -> p (j w)"), src).then_inc(xe_ld[k], 16)
                    wait(sp, wsp, g - 1)
                    wait(sp, y_ok, e * CE + (E_BASE[layer] - CE) if not isinstance(e, int) or e > 1 else 0)
                    if isinstance(e, int):
                        a, b, c = wg[e], wu[e], wd[e]
                    else:
                        a = wg[bass.ds(e, 1)].rearrange("o p f -> (o p) f")
                        b = wu[bass.ds(e, 1)].rearrange("o p f -> (o p) f")
                        c = wd[bass.ds(e, 1)].rearrange("o p f -> (o p) f")
                    load_mlp(sp, k, a, b, c, we_ld[k])
                for e in range(2):
                    f(e, e, 0)
                for it in range(1, E // 2):
                    for k in range(2):
                        f(it * 2 + k, k, it)

            def sp_c(phase):
                for i in range(RING):
                    sp.wait_ge(ysc[i], 32 * E * (phase + 1))
                for k in range(2):
                    sp.wait_ge(sv[k], 16 * (NB // 2) * (phase + 1))

                def f(m, k, u):
                    g = m + NB * phase
                    wait(sp, x1_ok, g - 1)
                    src = saved[phase][m] if isinstance(m, int) else \
                        saved[phase][bass.ds(m, 1)].rearrange("o p w -> (o p) w")
                    sp.dma_start(bc[k][:], src).then_inc(c_ld[k], 16)
                    ysrc = yr_v[m] if isinstance(m, int) else yr_v[bass.ds(m, 1)].rearrange("o p j w -> (o p) j w")
                    sp.dma_start(yin[k][:].rearrange("p j k d -> p j (k d)"), ysrc).then_inc(c_ld[k], 16)
                return f

            sp.wait_ge(fill_y, 32)
            sp_e(0)
            run_steps(sp, [(sp_c(0), 0), (save(1), 2)], NB, 2)
            sp_e(1)

            def sp_out(m, k, u):
                sp.wait_ge(x1_ok, m + (NB + 1))
                dst = out_v[m] if isinstance(m, int) else out_v[bass.ds(m, 1)].rearrange("o p j d -> (o p) j d")
                sp.dma_start(dst, x1[k][:]).then_inc(out_ok[k], 16)

            run_steps(sp, [(sp_c(1), 0), (sp_out, 1)], NB, 2)
            for k in range(2):
                sp.wait_ge(out_ok[k], 16 * (NB // 2))

        @block.gpsimd
        def _(pool):
            nc.gpsimd.memset(zero[:], 0.0).then_inc(zeroed, 1)

            def scatter_rows(layer):
                if layer == 0:
                    pool.wait_ge(fill_s, 16 * N_FILL)

                def f(r, k, u):
                    wait_alone(pool, idx_ok, r + (NB * layer + 1))
                    for j in range(TB):
                        for c in range(2):
                            nc.gpsimd.indirect_dma_start(
                                out=slots, out_offset=bass.IndirectOffsetOnAxis(ap=slot_i[k][:, j, c:c + 1], axis=0),
                                in_=stg[k][:, j, :], in_offset=None, bounds_check=E * CAP - 1,
                                oob_is_err=False).then_inc(scat[k], 16)
                return f

            def scatter_results(layer):
                def f(c, k, u):
                    if k % CE == 0:
                        wait_alone(pool, ri_ch, (u * 2 + k // CE) * 3 + (3 * E * layer + 3))
                    wait_alone(pool, y_cp, c + (E_BASE[layer] + 1))
                    for t in range(2):
                        nc.gpsimd.indirect_dma_start(
                            out=yrows,
                            out_offset=bass.IndirectOffsetOnAxis(
                                ap=row_i[k // CE][:, 2 * (k % CE) + t:2 * (k % CE) + t + 1], axis=0),
                            in_=yst[k % RING][:, t, :], in_offset=None, bounds_check=TOPK * NTOK - 1,
                            oob_is_err=False).then_inc(ysc[k % RING], 16)
                return f

            def add_bias(m, k, u):
                pool.wait_ge(x1_ok, m + 1)
                wait(pool, x_dv, (m - 1) * TB if not isinstance(m, int) or m > 1 else 0)
                nc.gpsimd.tensor_tensor(x1b[k][:], x1[k][:],
                                        bvr[:, :].rearrange("p (o d) -> p o d", o=1).broadcast_to([P, TB, D]),
                                        ALU.add).then_inc(x1b_ok, 1)

            run_steps(pool, [(scatter_rows(0), 0)], NB, 2)
            run_steps(pool, [(scatter_results(0), 0)], NCH, 2 * CE)
            run_steps(pool, [(add_bias, 0), (scatter_rows(1), 2)], NB, 2)
            run_steps(pool, [(scatter_results(1), 0)], NCH, 2 * CE)

        @block.scalar
        def _(act):
            def apply_norm(which, src, dst, g):
                act.wait_ge(ln_ok[which], g + 1)
                wait(act, lo_ok[which], g * 2)
                for j in range(TB):
                    nc.scalar.activation(dst[:, j, :], src[:, j, :], ACT.Identity, bias=nmr[which][:, j:j + 1],
                                         scale=rs[which][:, 0, j:j + 1]).then_inc(xn_ok[which], 1)
                act.wait_ge(xn_ok[which], (g + 1) * TB)

            def r_norm(layer):
                def f(r, k, u):
                    apply_norm(0, X[k], xnr, r + NB * layer)
                    wait(act, scat[k], (u + (NB // 2) * layer) * (16 * 2 * TB))
                    nc.scalar.copy(hi_of(stg[k][:, :, :]), xnr[:]).then_inc(hi_ok[0], 1)
                return f

            def r_xt(layer):
                def f(r, k, u):
                    c0 = r * CB + R_BASE[layer]
                    for i in range(CB):
                        act.wait_ge(t_ok, c0 + (i + 1))
                        if i == 0:
                            wait(act, gu_ok, c0)
                        nc.scalar.copy(xtr[:, :, i * CH:(i + 1) * CH], psT).then_inc(xt_ok, 1)
                return f

            def r_exp(layer):
                def f(r, k, u):
                    act.wait_ge(dl_ok, r + (NB * layer + 1))
                    nc.scalar.activation(ex[:], dl[:], ACT.Exp).then_inc(ex_ok, 1)
                return f

            def silu(c, par):
                act.wait_ge(gu_ok, c + 1)
                nc.scalar.activation(sA[par][:], psGU[par][:, 0, :], ACT.Silu, scale=1.0 / WS)
                nc.scalar.activation(sB[par][UB:UB + FB, :], psR[par][0:FB, :], ACT.Silu,
                                     scale=1.0 / WS).then_inc(silu_ok, 1)

            def r_mlp(layer):
                def f(r, k, u):
                    for i in range(CB):
                        silu(r * CB + (R_BASE[layer] + i), i % 2)
                return f

            def e_t(layer):
                def f(c, k, u):
                    g = c + E_BASE[layer]
                    act.wait_ge(t_ok, g + 1)
                    act.wait_ge(gu_ok, g - 1)
                    nc.scalar.copy(xte[k % 2][:], psT).then_inc(xt_ok, 1)
                return f

            def e_silu(layer):
                def f(c, k, u):
                    silu(c + E_BASE[layer], k % 2)
                return f

            def e_out(layer):
                def f(c, k, u):
                    act.wait_ge(y_ok, c + (E_BASE[layer] + 1))
                    wait(act, ysc[k % RING], (u * 2 + k // RING + E * layer) * 32)
                    nc.scalar.activation(yst[k % RING][:], psY, ACT.Copy, scale=0.5).then_inc(y_cp, 1)
                return f

            def c_norm(m, k, u):
                apply_norm(1, x1[k], xnc, m)
                nc.scalar.copy(hlc[:, 0], xnc[:]).then_inc(hi_ok[1], 1)

            def c_xt(m, k, u):
                for i in range(CB):
                    act.wait_ge(tc_ok, m * CB + (i + 1))
                    if i == 0:
                        wait(act, v_ok, (m - 1) * 4)
                    nc.scalar.copy(xtc[k][:, :, BL + i * CH:BL + (i + 1) * CH],
                                   psTC[i % 2]).then_inc(xtc_ok, 1)
                for h in range(2):
                    act.wait_ge(qk_ok, m * 2 + (h + 1))
                    if h == 0:
                        wait(act, s_ok, (m - 1) * 4)
                    c = slice(h * 512, (h + 1) * 512)
                    nc.scalar.activation(qT[k][:, c], psGU[0][:].rearrange("p a c -> p (a c)"), ACT.Identity,
                                         bias=bcol[:, 0:1], scale=1.0 / WS)
                    nc.scalar.activation(kT[k][:, BL + h * 512:BL + (h + 1) * 512],
                                         psGU[1][:].rearrange("p a c -> p (a c)"), ACT.Identity,
                                         bias=bcol[:, 1:2], scale=1.0 / WS).then_inc(qk_cp, 1)

            def a_pair(i):
                def f(m, k, u):
                    n = m * 4 + i
                    act.wait_ge(v_ok, n + 1)
                    wait(act, o_ok, n - 1)
                    nc.scalar.activation(vs[i % 2][:].rearrange("p t w d -> p (t w d)"),
                                         psV.rearrange("p b d -> p (b d)"), ACT.Copy,
                                         scale=1.0 / WS).then_inc(v_cp, 1)
                    act.wait_ge(nm_ok, n + 1)
                    wait(act, pt_ok, n - 1)
                    wait(act, ri_ok, n - 1)
                    for t in range(2):
                        nc.scalar.activation(pr[i % 2][:, t, :], psS2[:, t, :], ACT.Exp,
                                             bias=nm[i % 2][:, t:t + 1], scale=ATT,
                                             accum_out=rsum[i % 2][:, t:t + 1]).then_inc(p_ok, 1)
                return f

            act.wait_ge(ld_w, 16 * N_LDW)
            run_steps(act, [(r_norm(0), 0), (r_mlp(0), 1), (r_xt(0), 0), (r_exp(0), 0)], NB, 2)
            run_steps(act, [(e_t(0), 3), (e_silu(0), 4), (e_out(0), 5)], NCH, 2 * CE)
            run_steps(act, [(r_norm(1), 2), (a_pair(0), 1), (c_norm, 0), (r_xt(1), 2), (a_pair(1), 1), (r_exp(1), 2),
                            (a_pair(2), 1), (a_pair(3), 1), (c_xt, 0), (r_mlp(1), 2)], NB, 2)
            run_steps(act, [(e_t(1), 3), (e_silu(1), 4), (e_out(1), 5)], NCH, 2 * CE)

        @block.tensor
        def _(pe):
            def transpose_chunk(dst, hi, lo, t0, ok):
                for t in range(2):
                    nc.tensor.transpose(dst[:, 0, t * P:(t + 1) * P], hi[:, t0 + t, :], idh[:])
                    last = nc.tensor.transpose(dst[:, 1, t * P:(t + 1) * P], lo[:, t0 + t, :], idh[:])
                last.then_inc(ok, 1)

            def three(dst, w_hi, w_lo, x_hi, x_lo, weights_first=True):
                for n, (a, b) in enumerate(((w_hi, x_hi), (w_hi, x_lo), (w_lo, x_hi))):
                    if not weights_first:
                        a, b = b, a
                    last = nc.tensor.matmul(dst, a, b, start=n == 0, stop=n == 2)
                return last

            def gate_up(c, par, w, xt, cols):
                wait(pe, h_ok, c - 1)
                g = ghl[w]
                for a in range(2):
                    three(psGU[par][:, a, :], g[:, 0, a * FA:(a + 1) * FA], g[:, 1, a * FA:(a + 1) * FA],
                          xt[:, 0, cols], xt[:, 1, cols])
                three(psR[par][0:GW - 2 * FA, :], g[:, 0, 2 * FA:GW], g[:, 1, 2 * FA:GW],
                      xt[:, 0, cols], xt[:, 1, cols]).then_inc(gu_ok, 1)

            def down(c, par, w):
                pe.wait_ge(h_ok, c + 1)
                wait(pe, y_cp, c)
                for t in range(2):
                    cols = slice(t * P, (t + 1) * P)
                    nc.tensor.matmul(psY[:, t, :], hA[par][:, cols], wdn[w][:, 0, :], start=True, stop=False)
                    last = nc.tensor.matmul(psY[:, t, :], hB[par][:, cols], wdn[w][:, 1, :],
                                            start=False, stop=True)
                last.then_inc(y_ok, 1)

            def r_t(layer):
                def f(r, k, u):
                    g = r + NB * layer
                    c0 = r * CB + R_BASE[layer]
                    pe.wait_ge(lo_ok[0], g * 2 + 1)
                    for i in range(CB):
                        wait(pe, xt_ok, c0 + i)
                        transpose_chunk(psT, hi_of(stg[k][:, :, :]), lo_of(stg[k][:, :, :]), 2 * i, t_ok)
                    pe.wait_ge(xt_ok, c0 + CB)
                    wait(pe, y_cp, c0)
                    for j in range(TB):
                        cols = slice(j * P, (j + 1) * P)
                        last = three(psL[:, j * E:(j + 1) * E], whl[:, 0, 3 * D:], whl[:, 1, 3 * D:],
                                     xtr[:, 0, cols], xtr[:, 1, cols], weights_first=False)
                    last.then_inc(lg_ok, 1)
                return f

            def r_pos(layer):
                def f(r, k, u):
                    g = r + NB * layer
                    pe.wait_ge(ohs_ok, g + 1)
                    wait(pe, rt2_ch, g * N_RT2)
                    first = isinstance(r, int) and r == 0
                    m = ohs[:, :, :].rearrange("p j e -> p (j e)")
                    last = nc.tensor.matmul(psPos, tri[:], m, start=True, stop=False)
                    for j in range(TB - 1):
                        last = nc.tensor.matmul(
                            psPos[:, (j + 1) * E:].rearrange("p (j e) -> p j e", e=E), one[:],
                            ohs[:, j:j + 1, :].broadcast_to([P, TB - 1 - j, E]), start=False,
                            stop=first and j == TB - 2)
                    if not first:
                        last = nc.tensor.matmul(psPos.rearrange("p (j e) -> p j e", e=E), one[:],
                                                maccb[:, :].rearrange("p (o e) -> p o e", o=1)
                                                .broadcast_to([P, TB, E]), start=False, stop=True)
                    last.then_inc(pos_ok, 1)
                return f

            def counts(layer):
                pe.wait_ge(rt2_ch, NB * (layer + 1) * N_RT2)
                pe.wait_ge(y_cp, NB * CB + R_BASE[layer])
                nc.tensor.matmul(psPos[:, 0:E], one[:], maccb[:], start=True, stop=True).then_inc(cnt_mm, 1)
                pe.wait_ge(cnt_ok, layer + 1)

            def r_mlp(layer):
                def f(r, k, u):
                    c0 = r * CB + R_BASE[layer]
                    if layer:
                        late = isinstance(r, int)
                        pe.wait_ge(qk_cp, min(2 * (r + 3), 2 * NB) if late else r * 2 + 6)
                        pe.wait_ge(v_cp, min(4 * (r + 2), 4 * NB) if late else r * 4 + 8)
                        pe.wait_ge(x_dv, min(TB * (r + 2), TB * NB) if late else r * TB + 2 * TB)
                    pe.wait_ge(rt2_ch, (r + NB * layer) * N_RT2 + 5)
                    for i in range(CB + 1):
                        if i < CB:
                            gate_up(c0 + i, i % 2, 2, xtr, slice(i * CH, (i + 1) * CH))
                        if i:
                            down(c0 + (i - 1), (i - 1) % 2, 2)
                return f

            def e_t(layer):
                def f(c, k, u):
                    g = c + E_BASE[layer]
                    if k % CE == 0:
                        pe.wait_ge(xe_ld[k // CE], (u + E // 2 * layer) * 16 + 16)
                    pe.wait_ge(xt_ok, g)
                    rows = xe[k // CE][:, :, :]
                    transpose_chunk(psT, hi_of(rows), lo_of(rows), 2 * (k % CE), t_ok)
                return f

            def e_gu(layer):
                def f(c, k, u):
                    g = c + E_BASE[layer]
                    pe.wait_ge(xt_ok, g + 1)
                    if k % CE == 0:
                        pe.wait_ge(wsp, u * 2 + (k // CE + E * layer + 1))
                    gate_up(g, k % 2, k // CE, xte[k % 2], slice(0, CH))
                return f

            def e_down(layer):
                def f(c, k, u):
                    if k % CE == 0:
                        pe.wait_ge(we_ld[k // CE], (u + E // 2 * layer) * 96 + 96)
                    down(c + E_BASE[layer], k % 2, k // CE)
                return f

            def c_t(m, k, u):
                pe.wait_ge(lo_ok[1], m * 2 + 2)
                wait(pe, p_ok, m * TB)
                wait(pe, pt_cp, m * 4)
                for i in range(CB):
                    wait(pe, xtc_ok, m * CB + (i - 1))
                    transpose_chunk(psTC[i % 2], hlc[:, 0], hlc[:, 1], 2 * i, tc_ok)
                for h in range(2):
                    pe.wait_ge(xtc_ok, m * CB + (2 * h + 2))
                    wait(pe, qk_cp, m * 2 + h)
                    if h == 0:
                        pe.wait_ge(h_ok, max(R_BASE[1], R_BASE[1] + CB * (m - 2)) if isinstance(m, int)
                                   else m * CB + (R_BASE[1] - 2 * CB))
                    cols = slice(BL + h * 512, BL + (h + 1) * 512)
                    for a in range(2):
                        last = three(psGU[a][:].rearrange("p a c -> p (a c)"), whl[:, 0, a * D:(a + 1) * D],
                                     whl[:, 1, a * D:(a + 1) * D], xtc[k][:, 0, cols], xtc[k][:, 1, cols])
                    last.then_inc(qk_ok, 1)

            def a_pair(i):
                def f(m, k, u):
                    n = m * 4 + i
                    if i == 0:
                        pe.wait_ge(qk_cp, m * 2 + 2)
                        pe.wait_ge(h_ok, max(R_BASE[1], R_BASE[1] + CB * (m - 1)) if isinstance(m, int)
                                   else m * CB + (R_BASE[1] - CB))
                    wait(pe, p_ok, n * 2)
                    for t in range(2):
                        j = 2 * i + t
                        mk = 0 if j == 0 else 2 if j == TB - 1 else 1
                        nc.tensor.matmul(psS2[:, t, :], blk[:], msk[:, mk, :], start=True, stop=False)
                        last = nc.tensor.matmul(psS2[:, t, :], qT[k][:, j * P:(j + 1) * P],
                                                kT[k][:, j * P:j * P + WIN], start=False, stop=True)
                    last.then_inc(s_ok, 1)
                    wait(pe, v_cp, n)
                    for t in range(2):
                        for w in range(2):
                            o = (2 * i + t) * P + w * HW_
                            last = three(psV[:, 2 * t + w, :],
                                         whl[:, 0, 2 * D:3 * D], whl[:, 1, 2 * D:3 * D],
                                         xtc[k][:, 0, o:o + HW_], xtc[k][:, 1, o:o + HW_], weights_first=False)
                    last.then_inc(v_ok, 1)
                    pe.wait_ge(p_ok, n * 2 + 2)
                    wait(pe, pt_cp, n)
                    for t in range(2):
                        for w in range(2):
                            last = nc.tensor.transpose(psPT[:, t, w, :], pr[i % 2][:, t, w * HW_:(w + 1) * HW_],
                                                       cst[:, K_ID:K_ID + P])
                    last.then_inc(pt_ok, 1)
                    pe.wait_ge(pt_cp, n + 1)
                    pe.wait_ge(v_cp, n + 1)
                    wait(pe, x_dv, n * 2)
                    for t in range(2):
                        for w in range(2):
                            last = nc.tensor.matmul(psO[:, t, :], pts[i % 2][:, t, w, :], vs[i % 2][:, t, w, :],
                                                    start=w == 0, stop=w == 1)
                    last.then_inc(o_ok, 1)
                return f

            pe.wait_ge(split0, N_SPLIT0)
            run_steps(pe, [(r_mlp(0), 1), (r_t(0), 0), (r_pos(0), 0)], NB, 2)
            counts(0)
            run_steps(pe, [(e_t(0), 3), (e_gu(0), 4), (e_down(0), 5)], NCH, 2 * CE)
            run_steps(pe, [(a_pair(0), 1), (r_t(1), 2), (a_pair(1), 1), (r_pos(1), 2),
                           (a_pair(2), 1), (a_pair(3), 1), (c_t, 0), (r_mlp(1), 2)], NB, 2)
            counts(1)
            run_steps(pe, [(e_t(1), 3), (e_gu(1), 4), (e_down(1), 5)], NCH, 2 * CE)

        @block.vector
        def _(dve):
            def split(dst, src):
                nc.vector.tensor_scalar(dst[:, 0], src, WS, None, ALU.mult).then_inc(sp_ch, 1)
                sp_n[0] += 1
                dve.wait_ge(sp_ch, sp_n[0])
                return nc.vector.scalar_tensor_tensor(out=dst[:, 1], in0=src, scalar=WS, in1=dst[:, 0],
                                                      op0=ALU.mult, op1=ALU.subtract)

            sp_n = [0]

            for i in range(3):
                nc.vector.memset(gst[i][:], 0.0)
                nc.vector.memset(wdn[i][:], 0.0).then_inc(pad_ch, 1)
            dve.wait_ge(pad_ch, 3)
            nc.vector.memset(hB[0][:], 0.0).then_inc(pads, 1)
            nc.vector.memset(hB[1][:], 0.0)
            for k in range(2):
                nc.vector.memset(xtc[k][:], 0.0)
                nc.vector.memset(kT[k][:], 0.0)
            dve.wait_ge(ld_c, 16)
            nc.vector.tensor_copy(idh[:], cst[:, K_ID:K_ID + P])
            nc.vector.tensor_copy(tri[:], cst[:, K_TRI:K_TRI + P])
            nc.vector.tensor_copy(one[:], cst[:, K_ONE:K_ONE + P])
            nc.vector.tensor_copy(blk[:], cst[:, K_BLK:K_BLK + P])
            nc.vector.tensor_copy(msk[:].rearrange("p a c -> p (a c)"), cst[:, K_MASK:K_MASK + 3 * WIN])
            dve.wait_ge(ld_w, 16 * N_LDW)
            split(whl, wraw[:]).then_inc(split0, 1)
            split(ghl[2], gst[2][:]).then_inc(split0, 1)

            def norm(which, src, g):
                c = Chain(dve, ln_ch[which], N_LN, g)
                for j in range(TB):
                    c.add(nc.vector.bn_stats(st[which][:, j, :], src[:, j, :]))
                wait_alone(dve, ln_ch[which], c.base + TB)
                for j in range(TB):
                    c.add(nc.vector.bn_aggr(mv[which][:, j, :], st[which][:, j, :]))
                c.after()
                c.add(nc.vector.tensor_scalar(ve[which][:], mv[which][:, :, 1], EPS, None, ALU.add))
                c.after()
                a, b = nt[which][:, 0, :], nt[which][:, 1, :]
                y, y2 = rs[which][:, 0, :], rs[which][:, 1, :]
                c.add(nc.vector.tensor_single_scalar(a.bitcast(I32), ve[which][:, :].bitcast(I32), 1,
                                                     ALU.logical_shift_right))
                c.after()
                wait(dve, xn_ok[which], g * TB)
                c.add(nc.vector.tensor_scalar(y2.bitcast(I32), a.bitcast(I32), -1.0, float(MAGIC),
                                              ALU.mult, ALU.add))
                cur, nxt = y2, y
                for _ in range(3):
                    c.after()
                    c.add(nc.vector.tensor_tensor(a, cur, cur, ALU.mult))
                    c.after()
                    c.add(nc.vector.scalar_tensor_tensor(out=b, in0=a, scalar=-0.5, in1=ve[which][:],
                                                         op0=ALU.mult, op1=ALU.mult))
                    c.after()
                    c.add(nc.vector.scalar_tensor_tensor(out=nxt, in0=b, scalar=1.5, in1=cur,
                                                         op0=ALU.add, op1=ALU.mult))
                    cur, nxt = nxt, cur
                c.after()
                nc.vector.scalar_tensor_tensor(out=nmr[which][:], in0=mv[which][:, :, 0], scalar=-1.0, in1=cur,
                                               op0=ALU.mult, op1=ALU.mult).then_inc(ln_ok[which], 1)
                c.end()

            def r_norm(layer):
                def f(r, k, u):
                    if layer == 0:
                        dve.wait_ge(x_ld[k], u * 16 + 16)
                    else:
                        dve.wait_ge(x_dv, r * TB + TB)
                    norm(0, X[k], r + NB * layer)
                return f

            def r_lo(layer):
                def f(r, k, u):
                    g = r + NB * layer
                    dve.wait_ge(hi_ok[0], g + 1)
                    nc.vector.tensor_tensor(lo_of(stg[k][:, :, :]), xnr[:], hi_of(stg[k][:, :, :]),
                                            ALU.subtract).then_inc(lo_ok[0], 1)
                    wait(dve, sv[k], (u + (NB // 2) * layer) * 16)
                    nc.vector.scalar_tensor_tensor(out=base[k][:, 0:BT].rearrange("p (j d) -> p j d", d=D),
                                                   in0=xnr[:], scalar=0.5, in1=X[k][:], op0=ALU.mult,
                                                   op1=ALU.add).then_inc(lo_ok[0], 1)
                return f

            def r_route(layer):
                def f(r, k, u):
                    g = r + NB * layer
                    c = Chain(dve, rt_ch, N_RT, g)
                    dve.wait_ge(lg_ok, g + 1)
                    c.add(nc.vector.scalar_tensor_tensor(
                        out=lg[:, :, 0:E], in0=psL.rearrange("p (j e) -> p j e", e=E), scalar=1.0 / WS,
                        in1=rbr[:, :].rearrange("p (o e) -> p o e", o=1).broadcast_to([P, TB, E]),
                        op0=ALU.mult, op1=ALU.add))
                    wait_alone(dve, rt_ch, c.base + 1)
                    for j in range(TB):
                        c.add(nc.vector.max(m8[:, j, :], lg[:, j, 0:E]))
                    wait_alone(dve, rt_ch, c.base + 1 + TB)
                    for j in range(TB):
                        c.add(nc.vector.max_index(i8[:, j, :], m8[:, j, :], lg[:, j, 0:E]))
                    c.add(nc.vector.tensor_copy(lg[:, :, E:E + 1], m8[:, :, 1:2]))
                    c.after(2 * TB + 1)
                    c.add(nc.vector.tensor_tensor(
                        oh[:], i8[:, :, 0:2].rearrange("p j (k o) -> p j k o", o=1).broadcast_to([P, TB, 2, E]),
                        cst[:, K_IOTA:K_IOTA + E].rearrange("p (a b e) -> p a b e", a=1, b=1)
                        .broadcast_to([P, TB, 2, E]), ALU.is_equal))
                    c.after()
                    wait(dve, pos_ok, g)
                    nc.vector.tensor_tensor(ohs[:], oh[:, :, 0, :], oh[:, :, 1, :], ALU.add).then_inc(ohs_ok, 1)
                    wait(dve, ex_ok, g)
                    nc.vector.tensor_tensor(dl[:], lg[:], m8[:, :, 0:1].broadcast_to([P, TB, E + 1]),
                                            ALU.subtract).then_inc(dl_ok, 1)
                    if isinstance(r, int) and r == 0:
                        c.add(nc.vector.tensor_copy(t2run[:], cst[:, K_T2:K_T2 + TB]))
                    else:
                        c.add(nc.vector.tensor_scalar(t2run[:], t2run[:], float(2 * BT), None, ALU.add))
                    c.add(nc.vector.tensor_copy(stg[k][:, :, D + 1:D + 2], i8[:, :, 0:1]))
                    c.add(nc.vector.tensor_scalar(ec[:], i8[:, :, 0:2], float(CAP), None, ALU.mult))
                    c.after(c.n - 2)
                    c.add(nc.vector.tensor_copy(stg[k][:, :, D:D + 1].rearrange("p j o -> p (j o)"), t2run[:]))
                    c.end()
                return f

            def r_place(layer):
                def f(r, k, u):
                    g = r + NB * layer
                    c = Chain(dve, rt2_ch, N_RT2, g)
                    first = isinstance(r, int) and r == 0
                    dve.wait_ge(ex_ok, g + 1)
                    z, s, q = zz[:, 0, :], zz[:, 1, :], zz[:, 2, :]
                    c.add(nc.vector.tensor_reduce(z, ex[:, :, 0:E], AX_X, ALU.add))
                    c.add(nc.vector.tensor_reduce(mred[:], ohs[:, :, :].rearrange("p j e -> p e j"), AX_X,
                                                  ALU.add))
                    c.after(1)
                    c.add(nc.vector.reciprocal(pp[:, :, 0], z))
                    c.after(3)
                    c.add(nc.vector.tensor_tensor(pp[:, :, 1], ex[:, :, E], pp[:, :, 0], ALU.mult))
                    dve.wait_ge(pos_ok, g + 1)
                    c.add(nc.vector.tensor_tensor(
                        prod[:], oh[:], psPos.rearrange("p (j o e) -> p j o e", o=1, e=E)
                        .broadcast_to([P, TB, 2, E]), ALU.mult))
                    c.after(4)
                    c.add(nc.vector.scalar_tensor_tensor(out=s, in0=pp[:, :, 0], scalar=1e-9, in1=pp[:, :, 1],
                                                         op0=ALU.add, op1=ALU.add))
                    c.after(5)
                    c.add(nc.vector.tensor_reduce(pk[:], prod[:], AX_X, ALU.add))
                    c.after(6)
                    c.add(nc.vector.reciprocal(q, s))
                    if first:
                        c.add(nc.vector.tensor_copy(macc[:], mred[:]))
                    else:
                        c.add(nc.vector.tensor_tensor(macc[:], macc[:], mred[:], ALU.add))
                    c.after(7)
                    c.add(nc.vector.tensor_scalar(ov[:], pk[:], float(CAP), BIG, ALU.is_ge, ALU.mult))
                    c.add(nc.vector.tensor_tensor(s1[:], pk[:], ec[:], ALU.add))
                    c.after(8)
                    c.add(nc.vector.tensor_tensor(ww[:], pp[:], zz[:, 2, :].rearrange("p (j o) -> p j o", o=1)
                                                  .broadcast_to([P, TB, 2]), ALU.mult))
                    c.after(11)
                    wait(dve, scat[k], (u + (NB // 2) * layer) * (16 * 2 * TB))
                    nc.vector.tensor_tensor(slot_i[k][:], s1[:], ov[:], ALU.add).then_inc(idx_ok, 1)
                    c.add(nc.vector.tensor_copy(maccb[:], macc[:]))
                    c.after(12)
                    c.add(nc.vector.scalar_tensor_tensor(
                        out=base[k][:, BT:BW].rearrange("p (j k) -> p j k", k=2), in0=pk[:],
                        scalar=float(CAP), in1=ww[:], op0=ALU.is_lt, op1=ALU.mult))
                    c.end()
                return f

            def hidden(c, par):
                dve.wait_ge(silu_ok, c + 1)
                wait(dve, y_ok, c - 1)
                nc.vector.scalar_tensor_tensor(out=hA[par][:], in0=psGU[par][:, 1, :], scalar=1.0 / WS,
                                               in1=sA[par][:], op0=ALU.mult, op1=ALU.mult)
                nc.vector.scalar_tensor_tensor(out=hB[par][UB:UB + FB, :], in0=psR[par][UB:UB + FB, :],
                                               scalar=1.0 / WS, in1=sB[par][UB:UB + FB, :], op0=ALU.mult,
                                               op1=ALU.mult).then_inc(h_ok, 1)

            def r_mlp(layer):
                def f(r, k, u):
                    c0 = r * CB + R_BASE[layer]
                    for i in range(CB + 1):
                        if i < CB:
                            hidden(c0 + i, i % 2)
                        if i:
                            n = i - 1
                            dve.wait_ge(y_ok, c0 + (n + 1))
                            if n == 0:
                                dve.wait_ge(lo_ok[0], (r + (NB * layer + 1)) * 2)
                            b = base[k][:, n * CH:(n + 1) * CH]
                            nc.vector.scalar_tensor_tensor(
                                out=b, in0=psY.rearrange("p t d -> p (t d)"), scalar=0.5, in1=b,
                                op0=ALU.mult, op1=ALU.add).then_inc(y_cp, 1)
                return f

            def counts(layer):
                dve.wait_ge(cnt_mm, layer + 1)
                nc.vector.tensor_copy(cnt[:], psPos[:, 0:E]).then_inc(cnt_ok, 1)
                dve.wait_ge(cnt_ok, layer + 1)

            def e_prep(layer):
                def f(c, k, u):
                    if k % CE:
                        return
                    par = k // CE
                    e = u * 2 + par
                    g = e + E * layer
                    dve.wait_ge(we_ld[par], (u + E // 2 * layer) * 96 + 96)
                    wait(dve, gu_ok, e * CE + (E_BASE[layer] - CE) if not isinstance(e, int) or e > 1 else 0)
                    nc.vector.tensor_scalar(ghl[par][:, 0], gst[par][:], WS, None, ALU.mult).then_inc(esp_ch, 1)
                    dve.wait_ge(xe_ld[par], (u + E // 2 * layer) * 16 + 16)
                    ecol = slice(e, e + 1) if isinstance(e, int) else bass.ds(e, 1)
                    icol = slice(K_IOTA + e, K_IOTA + e + 1) if isinstance(e, int) else bass.ds(e + K_IOTA, 1)
                    wait(dve, ri_ch, g * 3)
                    nc.vector.tensor_scalar(inval[:], cst[:, K_POS:K_POS + JE], cnt[:, ecol], BIG,
                                            ALU.is_ge, ALU.mult).then_inc(ri_ch, 1)
                    nc.vector.scalar_tensor_tensor(
                        out=t2k[:], in0=xe[par][:, :, D + 1:D + 2].rearrange("p j o -> p (j o)"),
                        scalar=cst[:, icol], in1=xe[par][:, :, D:D + 1].rearrange("p j o -> p (j o)"),
                        op0=ALU.not_equal, op1=ALU.add).then_inc(ri_ch, 1)
                    dve.wait_ge(esp_ch, g + 1)
                    nc.vector.scalar_tensor_tensor(out=ghl[par][:, 1], in0=gst[par][:], scalar=WS,
                                                   in1=ghl[par][:, 0], op0=ALU.mult,
                                                   op1=ALU.subtract).then_inc(wsp, 1)
                    dve.wait_ge(ri_ch, g * 3 + 2)
                    for i in range(RING):
                        wait(dve, ysc[i], (g - 1) * 32)
                    nc.vector.tensor_tensor(row_i[par][:], inval[:], t2k[:], ALU.add).then_inc(ri_ch, 1)
                return f

            def e_h(layer):
                def f(c, k, u):
                    hidden(c + E_BASE[layer], k % 2)
                return f

            def c_combine(phase):
                def f(m, k, u):
                    g = m + NB * phase
                    c = Chain(dve, cb_ch, N_CB, g)
                    dve.wait_ge(c_ld[k], (u + (NB // 2) * phase) * 32 + 32)
                    if phase == 0:
                        wait(dve, x1b_ok, m - 1)
                        wait(dve, xn_ok[1], (m - 1) * TB if not isinstance(m, int) or m > 1 else 0)
                    else:
                        dve.wait_ge(x1b_ok, NB)
                        wait(dve, out_ok[k], u * 16)
                    w = bc[k][:, BT:BW]
                    for a in range(2):
                        for j in range(TB):
                            if a:
                                c.after(j + 1)
                            c.add(nc.vector.scalar_tensor_tensor(
                                out=x1[k][:, j, :], in0=yin[k][:, j, a, :], scalar=w[:, 2 * j + a:2 * j + a + 1],
                                in1=x1[k][:, j, :] if a else bc[k][:, j * D:(j + 1) * D], op0=ALU.mult, op1=ALU.add))
                    c.after()
                    nc.vector.tensor_copy(zz[:, 3, 0:1], cst[:, 0:1]).then_inc(x1_ok, 1)
                    c.end()
                return f

            def c_norm(m, k, u):
                norm(1, x1[k], m)

            def c_lo(m, k, u):
                dve.wait_ge(hi_ok[1], m + 1)
                nc.vector.tensor_tensor(hlc[:, 1], xnc[:], hlc[:, 0], ALU.subtract).then_inc(lo_ok[1], 2)

            def a_pair(i):
                def f(m, k, u):
                    n = m * 4 + i
                    b = i % 2
                    dve.wait_ge(s_ok, n + 1)
                    nc.vector.tensor_reduce(mx[b][:], psS2, AX_X, ALU.max).then_inc(mx_ok, 1)
                    dve.wait_ge(mx_ok, n + 1)
                    wait(dve, p_ok, (n - 1) * 2 if not isinstance(n, int) or n > 1 else 0)
                    nc.vector.tensor_scalar(nm[b][:], mx[b][:], -ATT, None, ALU.mult).then_inc(nm_ok, 1)
                    dve.wait_ge(p_ok, n * 2 + 2)
                    nc.vector.reciprocal(rinv[b][:], rsum[b][:]).then_inc(ri_ok, 1)
                    dve.wait_ge(pt_ok, n + 1)
                    wait(dve, o_ok, n - 1)
                    nc.vector.tensor_copy(pts[b][:], psPT).then_inc(pt_cp, 1)
                    dve.wait_ge(o_ok, n + 1)
                    if i == 0:
                        dve.wait_ge(x1b_ok, m + 1)
                        wait(dve, xn_ok[0], (m + (NB - 1)) * TB)
                    for t in range(2):
                        j = 2 * i + t
                        nc.vector.scalar_tensor_tensor(out=X[k][:, j, :], in0=psO[:, t, :],
                                                       scalar=rinv[b][:, t:t + 1], in1=x1b[k][:, j, :],
                                                       op0=ALU.mult, op1=ALU.add).then_inc(x_dv, 1)
                return f

            run_steps(dve, [(r_norm(0), 0), (r_lo(0), 0), (r_mlp(0), 1), (r_route(0), 0), (r_place(0), 0)], NB, 2)
            counts(0)
            run_steps(dve, [(e_prep(0), 0), (e_h(0), 4)], NCH, 2 * CE)
            run_steps(dve, [(r_norm(1), 2), (a_pair(0), 1), (c_combine(0), 0), (c_norm, 0), (r_lo(1), 2),
                            (a_pair(1), 1), (c_lo, 0), (r_route(1), 2), (r_place(1), 2), (a_pair(2), 1),
                            (a_pair(3), 1), (r_mlp(1), 2)], NB, 2)
            counts(1)
            run_steps(dve, [(e_prep(1), 0), (e_h(1), 4)], NCH, 2 * CE)
            run_steps(dve, [(c_combine(1), 0)], NB, 2)


N_LN = 2 * TB + 3 + 9
N_RT = 1 + 2 * TB + 2 + 4
N_RT2 = 14
N_CB = 2 * TB
N_LDW = 8 + 6
N_SPLIT0 = 2
N_FILL = 4


def constants():
    import numpy as np
    c = np.zeros((P, K_N), np.float32)
    i = np.arange(P)
    c[:, K_ID:K_ID + P] = np.eye(P)
    c[:, K_TRI:K_TRI + P] = i[:, None] < i[None, :]
    c[:, K_ONE:K_ONE + P] = 1
    for b in range(P // BL):
        c[b, K_BLK + BL * b:K_BLK + BL * (b + 1)] = 1
        for v in range(3):
            m = c[b, K_MASK + v * WIN:K_MASK + (v + 1) * WIN]
            m[:] = -1e30
            m[BL * b:BL * (b + 3)] = 0
            if v == 0:
                m[:BL] = -1e30
            if v == 2:
                m[WIN - BL:] = -1e30
    c[:, K_IOTA:K_IOTA + E] = np.arange(E)
    c[:, K_T2:K_T2 + TB] = 2 * (np.arange(TB)[None] * P + i[:, None])
    c[:, K_POS:K_POS + JE] = i[:, None] * JE + np.arange(JE)[None]
    return c


_INS = ['L0_attn_x', 'L0_attn_Wq', 'L0_attn_bq', 'L0_attn_Wk', 'L0_attn_bk', 'L0_attn_Wv', 'L0_attn_bv',
        'L0_ffn_router_w', 'L0_ffn_router_b', 'L0_ffn_w_gate', 'L0_ffn_w_up', 'L0_ffn_w_down',
        'L0_ffn_sw_gate', 'L0_ffn_sw_up', 'L0_ffn_sw_down']


def kernel(**inputs):
    import numpy as _np
    import concourse.bacc as _bacc
    from concourse.bass_utils import run_bass_kernel_spmd as _run

    nc = _bacc.Bacc("TRN2", target_bir_lowering=False, num_devices=1)
    arrays, args = {}, []
    for name in _INS:
        arrays[f"in_{name}"] = _np.ascontiguousarray(inputs[name])
    arrays["in_constants"] = constants()
    for name, a in arrays.items():
        args.append(nc.dram_tensor(name, a.shape, mybir.dt.from_np(a.dtype), kind="ExternalInput").ap())
    args.append(nc.dram_tensor("out_0", (NB, BT, D), F32, kind="ExternalOutput").ap())
    build(nc, *args)
    r = _run(nc, [arrays], core_ids=[0])
    return r.results[0]["out_0"]
```

```python
from contextlib import ExitStack

import concourse.bass as bass
from concourse import mybir

F32 = mybir.dt.float32
F16 = mybir.dt.float16
BF16 = mybir.dt.bfloat16
I32 = mybir.dt.int32
U32 = mybir.dt.uint32
ALU = mybir.AluOpType
ACT = mybir.ActivationFunctionType
AX_X = mybir.AxisListType.X

P = 128
D = 128
E = 16
TOPK = 2
F = 176
FA = 128
FB = F - FA
UB = 64
NTOK = 8 * 1024
CAP = -(-5 * NTOK * TOPK // (4 * E))
NB = 8
TB = 8
BT = TB * P
CH = 256
CB = BT // CH
CE = CAP // CH
JE = CAP // P
NCH = E * CE
SW = D + 2
BW = BT + 2 * TB
GW = 2 * FA + 112
BL = 32
WIN = P + 2 * BL
HW_ = WIN // 2
PADT = BT + 2 * BL
WS = 64.0
BIG = float(1 << 20)
MAGIC = 0x5F3759DF
EPS = 1e-5
ATT = float(1.0 / (D ** 0.5))
NX = 3
NXE = 3
ZW = 1024
RING = CE

K_ID, K_TRI, K_ONE, K_BLK = 0, 128, 256, 384
K_MASK = 512
K_IOTA = K_MASK + 3 * WIN
K_T2 = K_IOTA + E
K_POS = K_T2 + TB
K_N = K_POS + JE


ORDER_R = [("bs", 1, 2), ("si", 2, 2), ("yt", 0, 2), ("sc", 0, 2), ("hd", 2, 2), ("gu", 3, 2), ("hi", 0, 1),
           ("dn", 1, 2), ("lo", 0, 1), ("yt", 1, 2), ("bs", 0, 1), ("si", 3, 2), ("t", 0, 1), ("dn", 2, 2),
           ("hi", 1, 1), ("hd", 3, 2), ("xt", 0, 1), ("yt", 2, 2), ("sc", 1, 2), ("t", 1, 1), ("lo", 1, 1),
           ("xt", 1, 1), ("sc", 2, 2), ("t", 2, 1), ("sc", 3, 2), ("xt", 2, 1), ("t", 3, 1), ("xt", 3, 1),
           ("norm", 0, 0), ("lg", 0, 1), ("rt", 0, 1), ("gu", 0, 1), ("si", 0, 1), ("gu", 1, 1), ("pos", 0, 1),
           ("hd", 0, 1), ("gu", 2, 1), ("ex", 0, 1), ("pl", 0, 1), ("dn", 3, 2), ("yt", 3, 2), ("si", 1, 1),
           ("dn", 0, 1), ("hd", 1, 1)]
ORDER_M = [("pe", 2, 2), ("t", 2, 3), ("xt", 2, 3), ("pt", 2, 2), ("vc", 3, 2), ("t", 3, 3), ("x2", 1, 2),
           ("comb", 0, 0), ("s", 3, 2), ("pta", 2, 2), ("clo", 0, 1), ("xt", 3, 3), ("chi", 1, 1), ("yt", 0, 4),
           ("o", 2, 2), ("lg", 0, 3), ("mx", 3, 2), ("ct", 0, 1), ("gu", 2, 4), ("addb", 0, 1), ("iv", 2, 2),
           ("x2", 2, 2), ("rt", 0, 3), ("gu", 3, 4), ("cx", 0, 1), ("pe", 3, 2), ("dn", 1, 4), ("yt", 1, 4),
           ("si", 2, 4), ("si", 3, 4), ("hd", 2, 4), ("ct", 1, 1), ("clo", 1, 1), ("cx", 1, 1), ("hd", 3, 4),
           ("pt", 3, 2), ("iv", 3, 2), ("ex", 0, 3), ("ct", 2, 1), ("cd", 2, 1), ("pos", 0, 3), ("pl", 0, 3),
           ("qk", 0, 1), ("pta", 3, 2), ("qc", 0, 1), ("ct", 3, 1), ("o", 3, 2), ("x2", 3, 2), ("sc", 3, 4),
           ("s", 0, 1), ("cx", 3, 1), ("qk", 1, 1), ("mx", 0, 1), ("pe", 0, 1), ("qc", 1, 1), ("v", 0, 1),
           ("pt", 0, 1), ("vc", 0, 1), ("gu", 0, 3), ("gu", 1, 3), ("dn", 2, 4), ("pta", 0, 1), ("si", 0, 3),
           ("norm2", 0, 0), ("yt", 2, 4), ("s", 1, 1), ("hd", 0, 3), ("addb", 1, 1), ("sc", 0, 3), ("dn", 3, 4),
           ("si", 1, 3), ("mx", 1, 1), ("hd", 1, 3), ("hi", 0, 2), ("yt", 3, 4), ("v", 1, 1), ("vd", 1, 1),
           ("o", 0, 1), ("iv", 0, 1), ("x2", 0, 1), ("v", 2, 1), ("sc", 1, 3), ("bs", 0, 2), ("pe", 1, 1),
           ("iv", 1, 1), ("vd", 2, 1), ("hi", 1, 2), ("pl_lo", 0, 2), ("chi", 0, 0), ("pt", 1, 1), ("ptc", 1, 1),
           ("t", 0, 2), ("xd", 0, 2), ("s", 2, 1), ("o", 1, 1), ("dn", 0, 3), ("pl_lo", 1, 2), ("mx", 2, 1),
           ("t", 1, 2), ("v", 3, 1), ("xt", 1, 2), ("sc", 2, 3), ("bs", 1, 2)]
ORDER_E = [("prep", 0, 0), ("rows", 0, 4), ("et", 0, 3), ("exx", 0, 3), ("gu", 0, 4), ("si", 0, 4), ("hd", 0, 4), ("dn", 0, 5),
           ("eo", 0, 5), ("es", 0, 5)]
ORDER_F = [("comb", 0, 0), ("out", 0, 0)]


class At:

    def __init__(self):
        self.n = {name: 0 for name in ("t", "gu", "dn", "qk", "v", "o", "lg", "pos")}
        self.experts = False
        self.unit = {}

    def even(self):
        gu = self.n["gu"]
        return gu - 1 + gu % 2 if gu else 0

    def odd(self):
        return self.n["gu"] - self.n["gu"] % 2

    def step(self, name, item, part):
        if name in ("t", "ct", "et"):
            self.n["t"] += 1
            self.unit[name, item, part] = self.n["t"]
        elif name in self.n:
            self.n[name] += 1


def wait(eng, sem, value):
    if value > 0:
        eng.wait_ge(sem, value)


def run_steps(order, at, fns, n, first):
    for s in range(n + max(lag for _, _, lag in order)):
        for name, part, lag in order:
            item = s - lag + first
            here = 0 <= s - lag < n
            if name in fns and (here or name == "norm2"):
                fns[name](item, part)
            if here:
                at.step(name, item, part)


class Chain:

    def __init__(self, eng, sem, per_item, item):
        self.eng, self.sem, self.base, self.n = eng, sem, per_item * item, 0
        self.per_item = per_item

    def add(self, ins):
        self.n += 1
        return ins.then_inc(self.sem, 1)

    def after(self, n=None):
        wait(self.eng, self.sem, self.base + (self.n if n is None else n))

    def end(self):
        assert self.n == self.per_item, (self.n, self.per_item)


def build(nc, x, wpack, bcols, brow, mlps, consts, out):
    ctx = ExitStack()

    def sb(name, shape, dt=F32):
        return ctx.enter_context(nc.sbuf_tensor(name, shape, dt))

    def ps(name, shape, dt=F32):
        return ctx.enter_context(nc.psum_tensor(name, shape, dt))

    def sem(name):
        return ctx.enter_context(nc.semaphore(name))

    def sems(name, n):
        return [sem(f"{name}{i}") for i in range(n)]

    with ctx:
        slots = nc.dram_tensor("slots", (E * CAP, SW), F32, kind="Internal").ap()
        yrows = nc.dram_tensor("yrows", (TOPK * NTOK, D), F32, kind="Internal").ap()

        cst = sb("cst", [P, K_N])
        zero = sb("zero", [P, ZW])
        idh = sb("idh", [P, P], F16)
        tri = sb("tri", [P, P], BF16)
        one = sb("one", [P, P], BF16)
        blk = sb("blk", [P, P], BF16)
        msk = sb("msk", [P, 3, WIN], BF16)
        bcol = sb("bcol", [P, 2])
        bqs = sb("bqs", [P, 1])
        brw = sb("brw", [P, D + E])
        wraw = sb("wraw", [P, 3 * D + E])
        whl = sb("whl", [P, 2, 3 * D + E], F16)
        gst = [sb(f"gst{i}", [P, GW]) for i in range(3)]
        ghl = [sb(f"ghl{i}", [P, 2, GW], F16) for i in range(3)]
        wdn = [sb(f"wdn{i}", [P, 2, D]) for i in range(3)]
        st = [sb(f"st{i}", [P, TB, 6]) for i in "rc"]
        mv = [sb(f"mv{i}", [P, TB, 2]) for i in "rc"]
        ve = [sb(f"ve{i}", [P, TB]) for i in "rc"]
        nt = [sb(f"nt{i}", [P, 2, TB]) for i in "rc"]
        rs = [sb(f"rs{i}", [P, 2, TB]) for i in "rc"]
        nmr = [sb(f"nmr{i}", [P, TB]) for i in "rc"]
        X = [sb(f"X{i}", [P, TB, D]) for i in range(NX)]
        base = [sb(f"base{i}", [P, BW]) for i in range(NB)]
        xnr = sb("xnr", [P, TB, D])
        stg = [sb(f"stg{i}", [P, TB, SW]) for i in range(2)]
        xtr = [sb(f"xtr{i}", [P, 2, BT], F16) for i in range(2)]
        lg = sb("lg", [P, TB, E + 1])
        m8 = sb("m8", [P, TB, 8])
        i8 = sb("i8", [P, TB, 8], U32)
        oh = sb("oh", [P, TB, 2, E])
        ohs = sb("ohs", [P, TB, E], BF16)
        ec = sb("ec", [P, TB, 2])
        dl = sb("dl", [P, TB, E + 1])
        ex = sb("ex", [P, TB, E + 1])
        zz = sb("zz", [P, 3, TB])
        pp = sb("pp", [P, TB, 2])
        ww = sb("ww", [P, TB, 2])
        prod = sb("prod", [P, TB, 2, E])
        pk = sb("pk", [P, TB, 2])
        ov = sb("ov", [P, TB, 2])
        s1 = sb("s1", [P, TB, 2])
        slot_i = [sb(f"slot_i{i}", [P, TB, 2], I32) for i in range(2)]
        t2run = sb("t2run", [P, TB])
        mred = sb("mred", [P, E])
        macc = sb("macc", [P, E])
        maccb = sb("maccb", [P, E], BF16)
        cnt = sb("cnt", [P, E])
        sA = [sb(f"sA{i}", [P, CH]) for i in range(2)]
        sB = [sb(f"sB{i}", [P, CH]) for i in range(2)]
        hA = [sb(f"hA{i}", [P, CH]) for i in range(2)]
        hB = [sb(f"hB{i}", [P, CH]) for i in range(2)]
        xe = [sb(f"xe{i}", [P, JE, SW]) for i in range(NXE)]
        xte = [sb(f"xte{i}", [P, 2, CH], F16) for i in range(2)]
        yst = [sb(f"yst{i}", [P, 2, D]) for i in range(RING)]
        inval = sb("inval", [P, JE])
        t2k = sb("t2k", [P, JE])
        row_i = [sb(f"row_i{i}", [P, JE], I32) for i in range(2)]
        yin = [sb(f"yin{i}", [P, TB, 2, D]) for i in range(NY)]
        xnc = sb("xnc", [P, TB, D])
        hlc = sb("hlc", [P, 2, TB, D], F16)
        xtc = [sb(f"xtc{i}", [P, 2, PADT], F16) for i in range(2)]
        qT = [sb(f"qT{i}", [P, BT]) for i in range(2)]
        kT = [sb(f"kT{i}", [P, PADT]) for i in range(2)]
        nm = [sb(f"nm{i}", [P, 2]) for i in range(2)]
        pr = [sb(f"pr{i}", [P, 2, WIN]) for i in range(2)]
        rsum = [sb(f"rsum{i}", [P, 2]) for i in range(2)]
        rinv = [sb(f"rinv{i}", [P, 2]) for i in range(2)]
        pts = [sb(f"pts{i}", [HW_, 2, 2, P]) for i in range(2)]
        vs = [sb(f"vs{i}", [HW_, 2, 2, D]) for i in range(2)]

        psGU = [ps(f"psGU{i}", [P, 2, CH]) for i in range(2)]
        psR_ = [ps(f"psR{i}", [P, 512]) for i in range(2)]
        psT_ = ps("psT", [P, 1024], F16)
        psY_ = ps("psY", [P, 512])
        psS = ps("psS", [P, 512])
        psP = ps("psP", [P, 512])
        psR = [t[:, 0:CH] for t in psR_]
        psV = psR_[0][0:HW_, :].rearrange("p (b d) -> p b d", d=D)
        psO = psR_[1][:, 0:2 * D].rearrange("p (t d) -> p t d", t=2)
        psT = psT_[:, 0:2 * CH].rearrange("p (h c) -> p h c", h=2)
        psL = psY_[:, 0:TB * E]
        psPos = psY_[:, TB * E:2 * TB * E]
        psY = psY_[:, 2 * D:4 * D].rearrange("p (t d) -> p t d", t=2)
        psS2 = psS[:, 0:2 * WIN].rearrange("p (t c) -> p t c", t=2)
        psPT = psP[0:HW_, :].rearrange("p (t w q) -> p t w q", t=2, w=2)

        ld_c = sem("const_loaded")
        ld_w = sem("weights_loaded")
        zeroed = sem("zero_tile_ready")
        split0 = sem("fixed_weights_split")
        cst_ok = sem("constants_cast")
        padded = sem("windows_padded")
        sp_ch = sem("fixed_hi_done")
        fill_s = sems("slots_filled", JE)
        fill_y = sem("yrows_filled")
        x_ld = sems("x_loaded", NX)
        x_dv = sem("x2_done")
        ln_ch = sems("ln_chain", 2)
        ln_ok = sems("ln_stats_done", 2)
        xn_ok = sems("xn_done", 2)
        hi_ok = sems("hi_done", 2)
        lo_ok = sems("lo_done", 2)
        bs_ok = sem("base_done")
        t_ok = sem("transposed")
        xt_ok = sem("xt_copied")
        lg_ok = sem("logits_done")
        rt_ch = sem("route_chain")
        ohs_ok = sem("onehot_done")
        dl_ok = sem("delta_done")
        ex_ok = sem("exp_done")
        pos_ok = sem("positions_done")
        rt2_ch = sem("position_chain")
        idx_ok = sem("slot_index_done")
        cnt_mm = sem("count_summed")
        cnt_ok = sem("count_copied")
        scat = sems("rows_scattered", 2)
        gu_ok = sem("gate_up_done")
        silu_ok = sem("silu_done")
        h_ok = sem("hidden_done")
        y_ok = sem("mlp_out_done")
        y_cp = sem("mlp_out_taken")
        xe_ld = sems("slots_loaded", NXE)
        wg_ld = sems("gate_up_loaded", 2)
        wd_ld = sems("down_loaded", 2)
        wsp = sem("expert_split")
        esp_ch = sem("expert_hi_done")
        ri_ch = sem("row_chain")
        ysc = sems("results_scattered", RING)
        y_ld = sems("results_loaded", NY)
        cb_ch = sem("combine_chain")
        xb_ok = sem("v_bias_added")
        qk_ok = sem("qk_done")
        qk_cp = sem("qk_copied")
        v_ok = sem("v_done")
        v_cp = sem("v_copied")
        s_ok = sem("scores_done")
        nm_ok = sem("negmax_done")
        p_ok = sem("probs_done")
        pt_ok = sem("probs_transposed")
        pt_cp = sem("probs_t_copied")
        o_ok = sem("attention_done")
        ri_ok = sem("inverse_sum_done")
        out_ok = sems("out_stored", NX)

        x_v = x.rearrange("b (j p) d -> b p j d", p=P)
        out_v = out.rearrange("b (j p) d -> b p j d", p=P)
        slots_v = slots.rearrange("(e p j) w -> e p (j w)", e=E, p=P)
        slots_e = slots.rearrange("(e c) w -> e c w", e=E)
        yr_v = yrows.rearrange("(m j p k) d -> m p j (k d)", m=NB, j=TB, p=P)

        def hi_of(rows):
            return rows[:, :, 0:D // 2].bitcast(F16)

        def lo_of(rows):
            return rows[:, :, D // 2:D].bitcast(F16)

        def tiles(h):
            return slice(h * TB // 2, (h + 1) * TB // 2)

        def chunk(g, i):
            return g * CB + i + (NCH if g >= NB else 0)

        def run_all(pieces):
            at = At()
            fns = pieces(at)
            for layer in range(2):
                if layer == 0:
                    run_steps(ORDER_R, at, fns, NB, 0)
                else:
                    run_steps(ORDER_M, at, fns, NB, NB)
                fns["counts"](layer)
                at.experts = True
                run_steps(ORDER_E, at, fns, NCH, NCH * layer)
                at.experts = False
            run_steps(ORDER_F, at, fns, NB, 2 * NB)

        block = ctx.enter_context(nc.Block())

        @block.sync
        def _(sp):
            def load_x(g):
                wait(sp, bs_ok, 2 * (g - NX + 1))
                sp.dma_start(X[g % NX][:], x_v[g]).then_inc(x_ld[g % NX], 16)

            def load_gate_up(e, layer):
                g = e + E * layer
                wait(sp, wsp, g - 1)
                sp.dma_start(gst[e % 2][:], mlps[e][:, 0:GW]).then_inc(wg_ld[e % 2], 16)

            def load_down(e, layer):
                g = e + E * layer
                wait(sp, y_ok, chunk_end(g - 2))
                sp.dma_start(wdn[e % 2][:].rearrange("p a d -> p (a d)"),
                             mlps[e][:, GW:]).then_inc(wd_ld[e % 2], 16)

            def chunk_end(g):
                return 0 if g < 0 else (g + 1) * CE + NB * CB * (g // E + 1)

            load_x(0)
            sp.dma_start(cst[:], consts).then_inc(ld_c, 16)
            sp.dma_start(wraw[:], wpack).then_inc(ld_w, 16)
            sp.dma_start(bcol[:], bcols).then_inc(ld_w, 16)
            sp.dma_start(brw[:], brow.broadcast_to([P, D + E])).then_inc(ld_w, 16)
            sp.dma_start(gst[2][:], mlps[E][:, 0:GW]).then_inc(ld_w, 16)
            sp.dma_start(wdn[2][:].rearrange("p a d -> p (a d)"), mlps[E][:, GW:]).then_inc(ld_w, 16)
            sp.wait_ge(zeroed, 1)

            def fill(dst, s):
                sp.dma_start(dst, zero[:, 0:dst.shape[2]].rearrange("p (o w) -> p o w", o=1)
                             .broadcast_to(list(dst.shape))).then_inc(s, 16)

            for j in range(JE):
                fill(slots_e[:, j * P:(j + 1) * P, :].rearrange("e p w -> p e w"), fill_s[j])
                if j < 2:
                    load_x(j + 1)

            load_gate_up(0, 0)
            load_down(0, 0)
            load_gate_up(1, 0)
            load_down(1, 0)
            load_x(3)
            load_x(4)
            rows = yrows.rearrange("(p f a) w -> p f (a w)", p=P, f=N_FILL_Y * 4)
            for i in range(N_FILL_Y):
                fill(rows[:, 4 * i:4 * i + 4, :], fill_y)
                if i + 5 < NB:
                    load_x(i + 5)

            def experts(layer):
                for k in range(2):
                    sp.wait_ge(scat[k], 16 * 2 * TB * (NB // 2) * (layer + 1))
                for e in range(E):
                    g = e + E * layer
                    if g >= NXE:
                        wait(sp, xt_ok, unit_end[g - NXE])
                        wait(sp, ri_ch, (g - NXE + 1) * 3)
                    sp.dma_start(xe[g % NXE][:].rearrange("p j w -> p (j w)"),
                                 slots_v[e]).then_inc(xe_ld[g % NXE], 16)
                    if 1 <= e < E - 1:
                        load_gate_up(e + 1, layer)
                        load_down(e + 1, layer)

            def results(m, phase):
                g = m + NB * phase
                wait(sp, cb_ch, (g - NY + 1) * N_CB)
                sp.dma_start(yin[g % NY][:].rearrange("p j k d -> p j (k d)"), yr_v[m]).then_inc(y_ld[g % NY], 16)

            unit_end = [(e + 1) * CE + NB * CB + (2 * NB * CB if e >= E else 0) for e in range(2 * E)]

            experts(0)
            for i in range(RING):
                sp.wait_ge(ysc[i], 32 * E)
            for m in range(NB):
                results(m, 0)
            for e in range(2):
                load_gate_up(e, 1)
                load_down(e, 1)
            experts(1)
            for i in range(RING):
                sp.wait_ge(ysc[i], 64 * E)
            for m in range(NY - 1):
                results(m, 1)
            for m in range(NB):
                if m + NY - 1 < NB:
                    results(m + NY - 1, 1)
                sp.wait_ge(cb_ch, (m + NB + 1) * N_CB)
                sp.dma_start(out_v[m], X[m % NX][:]).then_inc(out_ok[m % NX], 16)
            for k in range(NX):
                sp.wait_ge(out_ok[k], 16 * len(range(k, NB, NX)))

        @block.gpsimd
        def _(pool):
            nc.gpsimd.memset(zero[:], 0.0).then_inc(zeroed, 1)
            for k in range(2):
                nc.gpsimd.memset(xtc[k][:], 0.0)
                nc.gpsimd.memset(kT[k][:], 0.0).then_inc(padded, 1)

            def pieces(at):
                def scatter_rows(g, q):
                    if q == 0:
                        if g == 1:
                            for i in range(JE):
                                pool.wait_ge(fill_s[i], 16)
                        pool.wait_ge(idx_ok, g + 1)
                    for j in range(2 * q, 2 * q + 2):
                        if g == 0:
                            pool.wait_ge(fill_s[j], 16)
                        for c in range(2):
                            nc.gpsimd.indirect_dma_start(
                                out=slots,
                                out_offset=bass.IndirectOffsetOnAxis(ap=slot_i[g % 2][:, j, c:c + 1], axis=0),
                                in_=stg[g % 2][:, j, :], in_offset=None, bounds_check=E * CAP - 1,
                                oob_is_err=False).then_inc(scat[g % 2], 16)

                def scatter_results(c, _):
                    if c % CE == 0:
                        if c == 0:
                            pool.wait_ge(fill_y, 16 * N_FILL_Y)
                        pool.wait_ge(ri_ch, (c // CE + 1) * 3)
                    layer = c // NCH
                    pool.wait_ge(y_cp, c + 1 + NB * CB * (layer + 1))
                    for t in range(2):
                        j = 2 * (c % CE) + t
                        nc.gpsimd.indirect_dma_start(
                            out=yrows,
                            out_offset=bass.IndirectOffsetOnAxis(ap=row_i[c // CE % 2][:, j:j + 1], axis=0),
                            in_=yst[c % RING][:, t, :], in_offset=None, bounds_check=TOPK * NTOK - 1,
                            oob_is_err=False).then_inc(ysc[c % RING], 16)

                def c_lo(g, h):
                    pool.wait_ge(hi_ok[1], 2 * (g - NB) + h + 1)
                    nc.gpsimd.tensor_tensor(hlc[:, 1, tiles(h), :], xnc[:, tiles(h), :], hlc[:, 0, tiles(h), :],
                                            ALU.subtract).then_inc(lo_ok[1], 1)

                def r_lo(g, h):
                    pool.wait_ge(hi_ok[0], 2 * g + h + 1)
                    nc.gpsimd.tensor_tensor(lo_of(stg[g % 2][:, tiles(h), :]), xnr[:, tiles(h), :],
                                            hi_of(stg[g % 2][:, tiles(h), :]), ALU.subtract).then_inc(lo_ok[0], 1)

                def add_bias(g, h):
                    pool.wait_ge(hi_ok[1], 2 * (g - NB) + h + 1)
                    nc.gpsimd.tensor_tensor(
                        X[(g - NB) % NX][:, tiles(h), :], X[(g - NB) % NX][:, tiles(h), :],
                        brw[:, 0:D].rearrange("p (o d) -> p o d", o=1).broadcast_to([P, TB // 2, D]),
                        ALU.add).then_inc(xb_ok, 1)

                return dict(sc=scatter_rows, es=scatter_results, clo=c_lo, pl_lo=r_lo, addb=add_bias, counts=lambda layer: None)

            run_all(pieces)

        @block.scalar
        def _(act):
            act.wait_ge(ld_c, 16)
            nc.scalar.copy(idh[:], cst[:, K_ID:K_ID + P]).then_inc(cst_ok, 1)
            nc.scalar.copy(tri[:], cst[:, K_TRI:K_TRI + P])
            nc.scalar.copy(one[:], cst[:, K_ONE:K_ONE + P])
            nc.scalar.copy(blk[:], cst[:, K_BLK:K_BLK + P])
            nc.scalar.copy(msk[:].rearrange("p a c -> p (a c)"), cst[:, K_MASK:K_MASK + 3 * WIN]).then_inc(cst_ok, 1)

            def pieces(at):
                def apply_norm(which, src, dst, h, n):
                    act.wait_ge(ln_ok[which], n + 1)
                    wait(act, lo_ok[which], 2 * n + h - 1)
                    for j in range(TB)[tiles(h)]:
                        nc.scalar.activation(dst[:, j, :], src[:, j, :], ACT.Identity, bias=nmr[which][:, j:j + 1],
                                             scale=rs[which][:, 0, j:j + 1]).then_inc(xn_ok[which], 1)
                    act.wait_ge(xn_ok[which], n * TB + (h + 1) * TB // 2)

                def r_hi(g, h):
                    wait(act, bs_ok, 2 * g + h - 1)
                    apply_norm(0, X[g % NB % NX], xnr, h, g)
                    wait(act, scat[g % 2], g // 2 * (16 * 2 * TB))
                    nc.scalar.copy(hi_of(stg[g % 2][:, tiles(h), :]), xnr[:, tiles(h), :]).then_inc(hi_ok[0], 1)

                def c_hi(g, h):
                    apply_norm(1, X[(g - NB) % NX], xnc, h, g - NB)
                    if g > NB:
                        act.wait_ge(t_ok, at.unit["ct", g - 1, 2 * h + 1])
                    nc.scalar.copy(hlc[:, 0, tiles(h), :], xnc[:, tiles(h), :]).then_inc(hi_ok[1], 1)

                def r_xt(g, i):
                    act.wait_ge(t_ok, at.unit["t", g, i])
                    if g >= 2:
                        act.wait_ge(gu_ok, chunk(g - 2, i) + 1)
                        act.wait_ge(lg_ok, g - 1)
                    nc.scalar.copy(xtr[g % 2][:, :, i * CH:(i + 1) * CH], psT).then_inc(xt_ok, 1)

                def r_exp(g, _):
                    act.wait_ge(dl_ok, g + 1)
                    nc.scalar.activation(ex[:], dl[:], ACT.Exp).then_inc(ex_ok, 1)

                def silu(g, _):
                    c = silus[0]
                    silus[0] += 1
                    act.wait_ge(gu_ok, c + 1)
                    wait(act, h_ok, c - 1)
                    nc.scalar.activation(sA[c % 2][:], psGU[c % 2][:, 0, :], ACT.Silu, scale=1.0 / WS)
                    nc.scalar.activation(sB[c % 2][UB:UB + FB, :], psR[c % 2][0:FB, :], ACT.Silu,
                                         scale=1.0 / WS).then_inc(silu_ok, 1)

                def e_xt(c, _):
                    act.wait_ge(t_ok, at.unit["et", c, 0])
                    act.wait_ge(gu_ok, c - 1 + NB * CB * (c // NCH + 1))
                    nc.scalar.copy(xte[c % 2][:], psT).then_inc(xt_ok, 1)

                def e_out(c, _):
                    act.wait_ge(y_ok, c + 1 + NB * CB * (c // NCH + 1))
                    wait(act, ysc[c % RING], c // RING * 32)
                    nc.scalar.activation(yst[c % RING][:], psY, ACT.Copy, scale=0.5).then_inc(y_cp, 1)

                def c_xt(g, i):
                    m = g - NB
                    act.wait_ge(padded, 2)
                    act.wait_ge(t_ok, at.unit["ct", g, i])
                    wait(act, v_ok, (m - 1) * 4)
                    nc.scalar.copy(xtc[m % 2][:, :, BL + i * CH:BL + (i + 1) * CH], psT).then_inc(xt_ok, 1)

                def qk_copy(g, h):
                    m = g - NB
                    if m == 0 and h == 0:
                        act.wait_ge(split0, 3)
                        act.wait_ge(padded, 2)
                    act.wait_ge(qk_ok, m * 2 + h + 1)
                    wait(act, s_ok, (m - 1) * 4)
                    nc.scalar.activation(qT[m % 2][:, h * 512:(h + 1) * 512],
                                         psGU[0][:].rearrange("p a c -> p (a c)"), ACT.Identity,
                                         bias=bqs[:, 0:1], scale=ATT / WS)
                    nc.scalar.activation(kT[m % 2][:, BL + h * 512:BL + (h + 1) * 512],
                                         psGU[1][:].rearrange("p a c -> p (a c)"), ACT.Identity,
                                         bias=bcol[:, 1:2], scale=1.0 / WS).then_inc(qk_cp, 1)

                def v_copy(g, i):
                    n = (g - NB) * 4 + i
                    act.wait_ge(v_ok, n + 1)
                    wait(act, o_ok, n - 1)
                    nc.scalar.activation(vs[i % 2][:].rearrange("p t w d -> p (t w d)"),
                                         psV.rearrange("p b d -> p (b d)"), ACT.Copy,
                                         scale=1.0 / WS).then_inc(v_cp, 1)

                def probs(g, i):
                    n = (g - NB) * 4 + i
                    act.wait_ge(nm_ok, n + 1)
                    wait(act, pt_ok, n - 1)
                    wait(act, ri_ok, n - 1)
                    for t in range(2):
                        nc.scalar.activation(pr[i % 2][:, t, :], psS2[:, t, :], ACT.Exp,
                                             bias=nm[i % 2][:, t:t + 1], scale=1.0,
                                             accum_out=rsum[i % 2][:, t:t + 1]).then_inc(p_ok, 1)

                def pt_copy(g, i):
                    n = (g - NB) * 4 + i
                    act.wait_ge(pt_ok, n + 1)
                    wait(act, o_ok, n - 1)
                    nc.scalar.copy(pts[i % 2][:], psPT).then_inc(pt_cp, 1)

                return dict(hi=r_hi, chi=c_hi, xt=r_xt, ex=r_exp, si=silu, exx=e_xt, eo=e_out, cx=c_xt,
                            qc=qk_copy, vc=v_copy, pe=probs, pta=pt_copy, counts=lambda layer: None)

            silus = [0]
            run_all(pieces)

        @block.tensor
        def _(pe):
            def three(dst, w_hi, w_lo, x_hi, x_lo, weights_first=True):
                for n, (a, b) in enumerate(((w_hi, x_hi), (w_hi, x_lo), (w_lo, x_hi))):
                    if not weights_first:
                        a, b = b, a
                    last = nc.tensor.matmul(dst, a, b, start=n == 0, stop=n == 2)
                return last

            pe.wait_ge(cst_ok, 2)

            def pieces(at):
                n = at.n

                def transposes(hi, lo, t0):
                    wait(pe, xt_ok, n["t"])
                    for t in range(2):
                        nc.tensor.transpose(psT[:, 0, t * P:(t + 1) * P], hi[:, t0 + t, :], idh[:])
                        last = nc.tensor.transpose(psT[:, 1, t * P:(t + 1) * P], lo[:, t0 + t, :], idh[:])
                    last.then_inc(t_ok, 1)

                def y_free():
                    wait(pe, y_cp, n["dn"])
                    wait(pe, rt_ch, (n["lg"] - 1) * N_RT + 1)
                    wait(pe, rt2_ch, (n["pos"] - 1) * N_RT2 + 5)

                def r_t(g, i):
                    pe.wait_ge(lo_ok[0], 2 * g + i // 2 + 1)
                    transposes(hi_of(stg[g % 2][:, :, :]), lo_of(stg[g % 2][:, :, :]), 2 * i)

                def c_t(g, i):
                    pe.wait_ge(lo_ok[1], 2 * (g - NB) + i // 2 + 1)
                    transposes(hlc[:, 0], hlc[:, 1], 2 * i)

                def e_t(c, _):
                    e = c // CE
                    if c % CE == 0:
                        pe.wait_ge(xe_ld[e % NXE], (e // NXE + 1) * 16)
                    rows = xe[e % NXE][:, :, :]
                    transposes(hi_of(rows), lo_of(rows), 2 * (c % CE))

                def r_logits(g, _):
                    pe.wait_ge(xt_ok, at.unit["t", g, CB - 1])
                    if g == 0:
                        pe.wait_ge(split0, 3)
                    y_free()
                    for j in range(TB):
                        cols = slice(j * P, (j + 1) * P)
                        last = three(psL[:, j * E:(j + 1) * E], whl[:, 0, 3 * D:], whl[:, 1, 3 * D:],
                                     xtr[g % 2][:, 0, cols], xtr[g % 2][:, 1, cols], weights_first=False)
                    last.then_inc(lg_ok, 1)

                def r_pos(g, _):
                    y_free()
                    pe.wait_ge(ohs_ok, g + 1)
                    first = g % NB == 0
                    m = ohs[:, :, :].rearrange("p j e -> p (j e)")
                    last = nc.tensor.matmul(psPos, tri[:], m, start=True, stop=False)
                    for j in range(TB - 1):
                        last = nc.tensor.matmul(
                            psPos[:, (j + 1) * E:].rearrange("p (j e) -> p j e", e=E), one[:],
                            ohs[:, j:j + 1, :].broadcast_to([P, TB - 1 - j, E]), start=False,
                            stop=first and j == TB - 2)
                    if not first:
                        pe.wait_ge(rt2_ch, g * N_RT2)
                        last = nc.tensor.matmul(psPos.rearrange("p (j e) -> p j e", e=E), one[:],
                                                maccb[:, :].rearrange("p (o e) -> p o e", o=1)
                                                .broadcast_to([P, TB, E]), start=False, stop=True)
                    last.then_inc(pos_ok, 1)

                def counts(layer):
                    pe.wait_ge(rt2_ch, NB * (layer + 1) * N_RT2)
                    y_free()
                    nc.tensor.matmul(psPos[:, 0:E], one[:], maccb[:], start=True, stop=True).then_inc(cnt_mm, 1)
                    pe.wait_ge(cnt_ok, layer + 1)

                def gate_up(item, i):
                    c = n["gu"]
                    if c == 0:
                        pe.wait_ge(split0, 3)
                    par = c % 2
                    if at.experts:
                        w, xt, cols = item // CE % 2, xte[item % 2], slice(0, CH)
                        if item % CE == 0:
                            pe.wait_ge(wsp, item // CE + 1)
                        pe.wait_ge(xt_ok, at.unit["et", item, 0])
                    else:
                        w, xt, cols = 2, xtr[item % 2], slice(i * CH, (i + 1) * CH)
                        pe.wait_ge(xt_ok, at.unit["t", item, i])
                    wait(pe, h_ok, c - 1)
                    wait(pe, qk_cp, n["qk"])
                    if par == 0:
                        wait(pe, v_cp, n["v"])
                    else:
                        wait(pe, x_dv, 2 * n["o"])
                    hl = ghl[w]
                    for a in range(2):
                        three(psGU[par][:, a, :], hl[:, 0, a * FA:(a + 1) * FA], hl[:, 1, a * FA:(a + 1) * FA],
                              xt[:, 0, cols], xt[:, 1, cols])
                    three(psR[par][0:GW - 2 * FA, :], hl[:, 0, 2 * FA:GW], hl[:, 1, 2 * FA:GW],
                          xt[:, 0, cols], xt[:, 1, cols]).then_inc(gu_ok, 1)

                def down(item, i):
                    c = n["dn"]
                    par = c % 2
                    w = item // CE % 2 if at.experts else 2
                    if at.experts and item % CE == 0:
                        pe.wait_ge(wd_ld[w], (item // CE // 2 + 1) * 16)
                    pe.wait_ge(h_ok, c + 1)
                    y_free()
                    for t in range(2):
                        cols = slice(t * P, (t + 1) * P)
                        nc.tensor.matmul(psY[:, t, :], hA[par][:, cols], wdn[w][:, 0, :], start=True, stop=False)
                        last = nc.tensor.matmul(psY[:, t, :], hB[par][:, cols], wdn[w][:, 1, :],
                                                start=False, stop=True)
                    last.then_inc(y_ok, 1)

                def qk(g, h):
                    m = g - NB
                    pe.wait_ge(xt_ok, at.unit["ct", g, 2 * h + 1])
                    wait(pe, qk_cp, n["qk"])
                    wait(pe, h_ok, n["gu"])
                    cols = slice(BL + h * 512, BL + (h + 1) * 512)
                    for a in range(2):
                        last = three(psGU[a][:].rearrange("p a c -> p (a c)"), whl[:, 0, a * D:(a + 1) * D],
                                     whl[:, 1, a * D:(a + 1) * D], xtc[m % 2][:, 0, cols], xtc[m % 2][:, 1, cols])
                    last.then_inc(qk_ok, 1)

                def scores(g, i):
                    m = g - NB
                    pe.wait_ge(qk_cp, m * 2 + (1 if i == 0 else 2))
                    wait(pe, p_ok, (m * 4 + i) * 2)
                    for t in range(2):
                        j = 2 * i + t
                        mk = 0 if j == 0 else 2 if j == TB - 1 else 1
                        nc.tensor.matmul(psS2[:, t, :], blk[:], msk[:, mk, :], start=True, stop=False)
                        last = nc.tensor.matmul(psS2[:, t, :], qT[m % 2][:, j * P:(j + 1) * P],
                                                kT[m % 2][:, j * P:j * P + WIN], start=False, stop=True)
                    last.then_inc(s_ok, 1)

                def values(g, i):
                    m = g - NB
                    wait(pe, v_cp, n["v"])
                    wait(pe, h_ok, at.even())
                    for t in range(2):
                        for w in range(2):
                            o = (2 * i + t) * P + w * HW_
                            last = three(psV[:, 2 * t + w, :],
                                         whl[:, 0, 2 * D:3 * D], whl[:, 1, 2 * D:3 * D],
                                         xtc[m % 2][:, 0, o:o + HW_], xtc[m % 2][:, 1, o:o + HW_],
                                         weights_first=False)
                    last.then_inc(v_ok, 1)

                def probs_t(g, i):
                    k = (g - NB) * 4 + i
                    pe.wait_ge(p_ok, k * 2 + 2)
                    wait(pe, pt_cp, k)
                    for t in range(2):
                        for w in range(2):
                            last = nc.tensor.transpose(psPT[:, t, w, :], pr[i % 2][:, t, w * HW_:(w + 1) * HW_],
                                                       cst[:, K_ID:K_ID + P])
                    last.then_inc(pt_ok, 1)

                def attend(g, i):
                    k = (g - NB) * 4 + i
                    pe.wait_ge(pt_cp, k + 1)
                    pe.wait_ge(v_cp, k + 1)
                    wait(pe, x_dv, 2 * n["o"])
                    wait(pe, h_ok, at.odd())
                    for t in range(2):
                        for w in range(2):
                            last = nc.tensor.matmul(psO[:, t, :], pts[i % 2][:, t, w, :], vs[i % 2][:, t, w, :],
                                                    start=w == 0, stop=w == 1)
                    last.then_inc(o_ok, 1)

                return dict(t=r_t, ct=c_t, et=e_t, lg=r_logits, pos=r_pos, gu=gate_up, dn=down, qk=qk, s=scores,
                            v=values, pt=probs_t, o=attend, counts=counts)

            run_all(pieces)

        @block.vector
        def _(dve):
            def split(dst, src, n):
                nc.vector.tensor_scalar(dst[:, 0], src, WS, None, ALU.mult).then_inc(sp_ch, 1)
                dve.wait_ge(sp_ch, n)
                nc.vector.scalar_tensor_tensor(out=dst[:, 1], in0=src, scalar=WS, in1=dst[:, 0],
                                               op0=ALU.mult, op1=ALU.subtract).then_inc(split0, 1)

            def prepare():
                for k in range(2):
                    nc.vector.memset(hB[k][:], 0.0)
                dve.wait_ge(ld_w, 16 * N_LDW)
                split(whl, wraw[:], 1)
                split(ghl[2], gst[2][:], 2)
                nc.vector.tensor_scalar(bqs[:], bcol[:, 0:1], ATT, None, ALU.mult).then_inc(split0, 1)

            def norm_steps(which, src, n):
                c = Chain(dve, ln_ch[which], N_LN, n)
                for j in range(TB):
                    c.add(nc.vector.bn_stats(st[which][:, j, :], src[:, j, :]))
                yield
                wait(dve, ln_ch[which], c.base + TB)
                for j in range(TB):
                    c.add(nc.vector.bn_aggr(mv[which][:, j, :], st[which][:, j, :]))
                yield
                c.after()
                c.add(nc.vector.tensor_scalar(ve[which][:], mv[which][:, :, 1], EPS, None, ALU.add))
                yield
                c.after()
                a, b = nt[which][:, 0, :], nt[which][:, 1, :]
                y, y2 = rs[which][:, 0, :], rs[which][:, 1, :]
                c.add(nc.vector.tensor_single_scalar(a.bitcast(I32), ve[which][:, :].bitcast(I32), 1,
                                                     ALU.logical_shift_right))
                yield
                c.after()
                wait(dve, xn_ok[which], n * TB)
                c.add(nc.vector.tensor_scalar(y2.bitcast(I32), a.bitcast(I32), -1.0, float(MAGIC),
                                              ALU.mult, ALU.add))
                cur, nxt = y2, y
                for _ in range(3):
                    yield
                    c.after()
                    c.add(nc.vector.tensor_tensor(a, cur, cur, ALU.mult))
                    yield
                    c.after()
                    c.add(nc.vector.scalar_tensor_tensor(out=b, in0=a, scalar=-0.5, in1=ve[which][:],
                                                         op0=ALU.mult, op1=ALU.mult))
                    yield
                    c.after()
                    c.add(nc.vector.scalar_tensor_tensor(out=nxt, in0=b, scalar=1.5, in1=cur,
                                                         op0=ALU.add, op1=ALU.mult))
                    cur, nxt = nxt, cur
                yield
                c.after()
                nc.vector.scalar_tensor_tensor(out=nmr[which][:], in0=mv[which][:, :, 0], scalar=-1.0, in1=cur,
                                               op0=ALU.mult, op1=ALU.mult).then_inc(ln_ok[which], 1)
                c.end()

            def pieces(at):
                n = at.n

                def norm(g, _):
                    dve.wait_ge(x_ld[g % NX], (g // NX + 1) * 16)
                    for _ in norm_steps(0, X[g % NX], g):
                        pass
                    if g == 0:
                        prepare()

                def norm2(g, _):
                    m, r = g - NB, g - 2
                    runs = []
                    if m < NB:
                        dve.wait_ge(cb_ch, (m + 1) * N_CB)
                        runs.append(norm_steps(1, X[m % NX], m))
                    if NB <= r < 2 * NB:
                        dve.wait_ge(x_dv, (r - NB + 1) * TB)
                        runs.append(norm_steps(0, X[r % NB % NX], r))
                    while runs:
                        for run in list(runs):
                            if next(run, 0) == 0:
                                runs.remove(run)

                def r_lo(g, h):
                    dve.wait_ge(hi_ok[0], 2 * g + h + 1)
                    nc.vector.tensor_tensor(lo_of(stg[g % 2][:, tiles(h), :]), xnr[:, tiles(h), :],
                                            hi_of(stg[g % 2][:, tiles(h), :]), ALU.subtract).then_inc(lo_ok[0], 1)

                def r_base(g, h):
                    dve.wait_ge(hi_ok[0], 2 * g + h + 1)
                    if g >= NB:
                        dve.wait_ge(cb_ch, (g - NB + 1) * N_CB)
                    nc.vector.scalar_tensor_tensor(
                        out=base[g % NB][:, h * BT // 2:(h + 1) * BT // 2].rearrange("p (j d) -> p j d", d=D),
                        in0=xnr[:, tiles(h), :], scalar=0.5, in1=X[g % NB % NX][:, tiles(h), :], op0=ALU.mult,
                        op1=ALU.add).then_inc(bs_ok, 1)

                def r_route(g, _):
                    k = g % 2
                    c = Chain(dve, rt_ch, N_RT, g)
                    dve.wait_ge(lg_ok, g + 1)
                    c.add(nc.vector.scalar_tensor_tensor(
                        out=lg[:, :, 0:E], in0=psL.rearrange("p (j e) -> p j e", e=E), scalar=1.0 / WS,
                        in1=brw[:, D:].rearrange("p (o e) -> p o e", o=1).broadcast_to([P, TB, E]),
                        op0=ALU.mult, op1=ALU.add))
                    if g == 0:
                        dve.wait_ge(ld_c, 16)
                    c.after()
                    for j in range(TB):
                        c.add(nc.vector.max(m8[:, j, :], lg[:, j, 0:E]))
                    c.after()
                    for j in range(TB):
                        c.add(nc.vector.max_index(i8[:, j, :], m8[:, j, :], lg[:, j, 0:E]))
                    c.add(nc.vector.tensor_copy(lg[:, :, E:E + 1], m8[:, :, 1:2]))
                    c.after()
                    wait(dve, ex_ok, g)
                    nc.vector.tensor_tensor(dl[:], lg[:], m8[:, :, 0:1].broadcast_to([P, TB, E + 1]),
                                            ALU.subtract).then_inc(dl_ok, 1)
                    c.add(nc.vector.tensor_tensor(
                        oh[:], i8[:, :, 0:2].rearrange("p j (k o) -> p j k o", o=1).broadcast_to([P, TB, 2, E]),
                        cst[:, K_IOTA:K_IOTA + E].rearrange("p (a b e) -> p a b e", a=1, b=1)
                        .broadcast_to([P, TB, 2, E]), ALU.is_equal))
                    c.after()
                    wait(dve, pos_ok, g)
                    nc.vector.tensor_tensor(ohs[:], oh[:, :, 0, :], oh[:, :, 1, :], ALU.add).then_inc(ohs_ok, 1)
                    if g % NB == 0:
                        c.add(nc.vector.tensor_copy(t2run[:], cst[:, K_T2:K_T2 + TB]))
                    else:
                        c.add(nc.vector.tensor_scalar(t2run[:], t2run[:], float(2 * BT), None, ALU.add))
                    c.add(nc.vector.tensor_copy(stg[k][:, :, D + 1:D + 2], i8[:, :, 0:1]))
                    c.add(nc.vector.tensor_scalar(ec[:], i8[:, :, 0:2], float(CAP), None, ALU.mult))
                    c.after(c.n - 2)
                    c.add(nc.vector.tensor_copy(stg[k][:, :, D:D + 1].rearrange("p j o -> p (j o)"), t2run[:]))
                    c.end()

                def r_place(g, _):
                    k = g % 2
                    c = Chain(dve, rt2_ch, N_RT2, g)
                    dve.wait_ge(ex_ok, g + 1)
                    z, s, q = zz[:, 0, :], zz[:, 1, :], zz[:, 2, :]
                    c.add(nc.vector.tensor_reduce(z, ex[:, :, 0:E], AX_X, ALU.add))
                    c.add(nc.vector.tensor_reduce(mred[:], ohs[:, :, :].rearrange("p j e -> p e j"), AX_X,
                                                  ALU.add))
                    c.after(1)
                    c.add(nc.vector.reciprocal(pp[:, :, 0], z))
                    c.after(3)
                    c.add(nc.vector.tensor_tensor(pp[:, :, 1], ex[:, :, E], pp[:, :, 0], ALU.mult))
                    dve.wait_ge(pos_ok, g + 1)
                    c.add(nc.vector.tensor_tensor(
                        prod[:], oh[:], psPos.rearrange("p (j o e) -> p j o e", o=1, e=E)
                        .broadcast_to([P, TB, 2, E]), ALU.mult))
                    c.after(4)
                    c.add(nc.vector.scalar_tensor_tensor(out=s, in0=pp[:, :, 0], scalar=1e-9, in1=pp[:, :, 1],
                                                         op0=ALU.add, op1=ALU.add))
                    c.after(5)
                    c.add(nc.vector.tensor_reduce(pk[:], prod[:], AX_X, ALU.add))
                    c.after(6)
                    c.add(nc.vector.reciprocal(q, s))
                    if g % NB == 0:
                        c.add(nc.vector.tensor_copy(macc[:], mred[:]))
                    else:
                        c.add(nc.vector.tensor_tensor(macc[:], macc[:], mred[:], ALU.add))
                    c.after(7)
                    c.add(nc.vector.tensor_scalar(ov[:], pk[:], float(CAP), BIG, ALU.is_ge, ALU.mult))
                    c.add(nc.vector.tensor_tensor(s1[:], pk[:], ec[:], ALU.add))
                    c.after(8)
                    c.add(nc.vector.tensor_tensor(ww[:], pp[:], zz[:, 2, :].rearrange("p (j o) -> p j o", o=1)
                                                  .broadcast_to([P, TB, 2]), ALU.mult))
                    c.after(11)
                    wait(dve, scat[k], g // 2 * (16 * 2 * TB))
                    nc.vector.tensor_tensor(slot_i[k][:], s1[:], ov[:], ALU.add).then_inc(idx_ok, 1)
                    c.add(nc.vector.tensor_copy(maccb[:], macc[:]))
                    c.after(12)
                    c.add(nc.vector.scalar_tensor_tensor(
                        out=base[g % NB][:, BT:BW].rearrange("p (j k) -> p j k", k=2), in0=pk[:],
                        scalar=float(CAP), in1=ww[:], op0=ALU.is_lt, op1=ALU.mult))
                    c.end()

                def hidden(item, _):
                    c = hids[0]
                    hids[0] += 1
                    par = c % 2
                    dve.wait_ge(silu_ok, c + 1)
                    wait(dve, y_ok, c - 1)
                    nc.vector.scalar_tensor_tensor(out=hA[par][:], in0=psGU[par][:, 1, :], scalar=1.0 / WS,
                                                   in1=sA[par][:], op0=ALU.mult, op1=ALU.mult)
                    nc.vector.scalar_tensor_tensor(out=hB[par][UB:UB + FB, :], in0=psR[par][UB:UB + FB, :],
                                                   scalar=1.0 / WS, in1=sB[par][UB:UB + FB, :], op0=ALU.mult,
                                                   op1=ALU.mult).then_inc(h_ok, 1)

                def take(g, i):
                    dve.wait_ge(y_ok, chunk(g, i) + 1)
                    dve.wait_ge(bs_ok, 2 * g + i // 2 + 1)
                    b = base[g % NB][:, i * CH:(i + 1) * CH]
                    nc.vector.scalar_tensor_tensor(
                        out=b, in0=psY.rearrange("p t d -> p (t d)"), scalar=0.5, in1=b,
                        op0=ALU.mult, op1=ALU.add).then_inc(y_cp, 1)

                def counts(layer):
                    dve.wait_ge(cnt_mm, layer + 1)
                    nc.vector.tensor_copy(cnt[:], psPos[:, 0:E]).then_inc(cnt_ok, 1)
                    dve.wait_ge(cnt_ok, layer + 1)

                def e_prep(item, _):
                    if item % CE:
                        return
                    g = item // CE
                    par = g % 2
                    dve.wait_ge(wg_ld[par], (g // 2 + 1) * 16)
                    wait(dve, gu_ok, (g - 1) * CE + NB * CB * ((g - 2) // E + 1) if g > 1 else 0)
                    nc.vector.tensor_scalar(ghl[par][:, 0], gst[par][:], WS, None, ALU.mult).then_inc(esp_ch, 1)
                    dve.wait_ge(esp_ch, g + 1)
                    nc.vector.scalar_tensor_tensor(out=ghl[par][:, 1], in0=gst[par][:], scalar=WS,
                                                   in1=ghl[par][:, 0], op0=ALU.mult,
                                                   op1=ALU.subtract).then_inc(wsp, 1)

                def e_rows(item, _):
                    if item % CE:
                        return
                    g = item // CE
                    e, par = g % E, g % 2
                    dve.wait_ge(xe_ld[g % NXE], (g // NXE + 1) * 16)
                    wait(dve, ri_ch, g * 3)
                    nc.vector.tensor_scalar(inval[:], cst[:, K_POS:K_POS + JE], cnt[:, e:e + 1], BIG,
                                            ALU.is_ge, ALU.mult).then_inc(ri_ch, 1)
                    nc.vector.scalar_tensor_tensor(
                        out=t2k[:], in0=xe[g % NXE][:, :, D + 1:D + 2].rearrange("p j o -> p (j o)"),
                        scalar=cst[:, K_IOTA + e:K_IOTA + e + 1],
                        in1=xe[g % NXE][:, :, D:D + 1].rearrange("p j o -> p (j o)"),
                        op0=ALU.not_equal, op1=ALU.add).then_inc(ri_ch, 1)
                    dve.wait_ge(ri_ch, g * 3 + 2)
                    for i in range(RING):
                        wait(dve, ysc[i], (g - 1) * 32)
                    nc.vector.tensor_tensor(row_i[par][:], inval[:], t2k[:], ALU.add).then_inc(ri_ch, 1)

                def combine(g, _):
                    b = g - NB
                    m = b % NB
                    c = Chain(dve, cb_ch, N_CB, b)
                    dve.wait_ge(y_cp, chunk(b, CB - 1) + 1)
                    dve.wait_ge(rt2_ch, (b + 1) * N_RT2)
                    dve.wait_ge(y_ld[b % NY], (b // NY + 1) * 16)
                    dve.wait_ge(bs_ok, 4 * NB if b >= NB else 2 * (NB + max(m - NX + 1, 0)))
                    if b >= NB:
                        wait(dve, out_ok[m % NX], m // NX * 16)
                    w = base[m][:, BT:BW]
                    for a in range(2):
                        for j in range(TB):
                            if a:
                                c.after(j + 1)
                            c.add(nc.vector.scalar_tensor_tensor(
                                out=X[m % NX][:, j, :], in0=yin[b % NY][:, j, a, :],
                                scalar=w[:, 2 * j + a:2 * j + a + 1],
                                in1=X[m % NX][:, j, :] if a else base[m][:, j * D:(j + 1) * D],
                                op0=ALU.mult, op1=ALU.add))
                    c.end()

                def neg_max(g, i):
                    k = (g - NB) * 4 + i
                    dve.wait_ge(s_ok, k + 1)
                    wait(dve, p_ok, (k - 1) * 2)
                    nc.vector.tensor_reduce(nm[i % 2][:], psS2, AX_X, ALU.max, negate=True).then_inc(nm_ok, 1)

                def pt_copy(g, i):
                    k = (g - NB) * 4 + i
                    dve.wait_ge(pt_ok, k + 1)
                    wait(dve, o_ok, k - 1)
                    nc.vector.tensor_copy(pts[i % 2][:], psPT).then_inc(pt_cp, 1)

                def v_copy(g, i):
                    k = (g - NB) * 4 + i
                    dve.wait_ge(v_ok, k + 1)
                    wait(dve, o_ok, k - 1)
                    nc.vector.tensor_scalar(vs[i % 2][:].rearrange("p t w d -> p (t w d)"),
                                            psV.rearrange("p b d -> p (b d)"), 1.0 / WS, None,
                                            ALU.mult).then_inc(v_cp, 1)

                def r_xt(g, i):
                    dve.wait_ge(t_ok, at.unit["t", g, i])
                    if g >= 2:
                        dve.wait_ge(gu_ok, chunk(g - 2, i) + 1)
                        dve.wait_ge(lg_ok, g - 1)
                    nc.vector.tensor_copy(xtr[g % 2][:, :, i * CH:(i + 1) * CH], psT).then_inc(xt_ok, 1)

                def c_xt(g, i):
                    m = g - NB
                    dve.wait_ge(padded, 2)
                    dve.wait_ge(t_ok, at.unit["ct", g, i])
                    wait(dve, v_ok, (m - 1) * 4)
                    nc.vector.tensor_copy(xtc[m % 2][:, :, BL + i * CH:BL + (i + 1) * CH], psT).then_inc(xt_ok, 1)

                def c_lo(g, h):
                    dve.wait_ge(hi_ok[1], 2 * (g - NB) + h + 1)
                    nc.vector.tensor_tensor(hlc[:, 1, tiles(h), :], xnc[:, tiles(h), :], hlc[:, 0, tiles(h), :],
                                            ALU.subtract).then_inc(lo_ok[1], 1)

                def inverse(g, i):
                    k = (g - NB) * 4 + i
                    dve.wait_ge(p_ok, k * 2 + 2)
                    wait(dve, x_dv, 2 * (k - 1))
                    nc.vector.reciprocal(rinv[i % 2][:], rsum[i % 2][:]).then_inc(ri_ok, 1)

                def x2(g, i):
                    m = g - NB
                    k = m * 4 + i
                    dve.wait_ge(ri_ok, k + 1)
                    dve.wait_ge(xb_ok, 2 * m + i // 2 + 1)
                    dve.wait_ge(o_ok, k + 1)
                    for t in range(2):
                        rows = X[m % NX][:, 2 * i + t, :]
                        nc.vector.scalar_tensor_tensor(out=rows, in0=psO[:, t, :], scalar=rinv[i % 2][:, t:t + 1],
                                                       in1=rows, op0=ALU.mult, op1=ALU.add).then_inc(x_dv, 1)

                return dict(norm=norm, norm2=norm2, lo=r_lo, bs=r_base, rt=r_route, pl=r_place, hd=hidden, yt=take,
                            counts=counts, prep=e_prep, rows=e_rows, comb=combine, mx=neg_max, ptc=pt_copy,
                            iv=inverse, x2=x2, vd=v_copy, xd=r_xt, cd=c_xt, cl=c_lo)

            hids = [0]
            run_all(pieces)


N_LN = 2 * TB + 2 + 10
N_RT = 1 + 2 * TB + 2 + 4
N_RT2 = 14
N_CB = 2 * TB
N_LDW = 5
N_FILL_Y = 4
NY = 3


def constants():
    import numpy as np
    c = np.zeros((P, K_N), np.float32)
    i = np.arange(P)
    c[:, K_ID:K_ID + P] = np.eye(P)
    c[:, K_TRI:K_TRI + P] = i[:, None] < i[None, :]
    c[:, K_ONE:K_ONE + P] = 1
    for b in range(P // BL):
        c[b, K_BLK + BL * b:K_BLK + BL * (b + 1)] = 1
        for v in range(3):
            m = c[b, K_MASK + v * WIN:K_MASK + (v + 1) * WIN]
            m[:] = -1e30
            m[BL * b:BL * (b + 3)] = 0
            if v == 0:
                m[:BL] = -1e30
            if v == 2:
                m[WIN - BL:] = -1e30
    c[:, K_IOTA:K_IOTA + E] = np.arange(E)
    c[:, K_T2:K_T2 + TB] = 2 * (np.arange(TB)[None] * P + i[:, None])
    c[:, K_POS:K_POS + JE] = i[:, None] * JE + np.arange(JE)[None]
    return c


_INS = ['L0_attn_x', 'L0_attn_Wq', 'L0_attn_bq', 'L0_attn_Wk', 'L0_attn_bk', 'L0_attn_Wv', 'L0_attn_bv',
        'L0_ffn_router_w', 'L0_ffn_router_b', 'L0_ffn_w_gate', 'L0_ffn_w_up', 'L0_ffn_w_down',
        'L0_ffn_sw_gate', 'L0_ffn_sw_up', 'L0_ffn_sw_down']


def layout(inputs):
    import numpy as np
    (x, wq, bq, wk, bk, wv, bv, rw, rb, wg, wu, wd, sg, su, sd) = [np.asarray(inputs[name]) for name in _INS]
    mlps = np.zeros((E + 1, P, GW + 2 * D), np.float32)
    for i in range(E + 1):
        g, u, d = (wg[i], wu[i], wd[i]) if i < E else (sg, su, sd)
        mlps[i, :, 0:FA] = g[:, 0:FA]
        mlps[i, :, FA:2 * FA] = u[:, 0:FA]
        mlps[i, :, 2 * FA:2 * FA + FB] = g[:, FA:]
        mlps[i, :, 2 * FA + UB:2 * FA + UB + FB] = u[:, FA:]
        mlps[i, :, GW:GW + D] = d[0:FA]
        mlps[i, UB:UB + FB, GW + D:] = d[FA:]
    return {"x": np.ascontiguousarray(x),
            "qkv_router": np.concatenate([wq, wk, wv, rw], axis=1),
            "qk_bias": np.stack([bq, bk], axis=1),
            "v_router_bias": np.concatenate([bv, rb])[None],
            "mlps": mlps,
            "constants": constants()}


def kernel(**inputs):
    import concourse.bacc as _bacc
    from concourse.bass_utils import run_bass_kernel_spmd as _run

    nc = _bacc.Bacc("TRN2", target_bir_lowering=False, num_devices=1)
    arrays = layout(inputs)
    args = [nc.dram_tensor(name, a.shape, mybir.dt.from_np(a.dtype), kind="ExternalInput").ap()
            for name, a in arrays.items()]
    args.append(nc.dram_tensor("out_0", (NB, BT, D), F32, kind="ExternalOutput").ap())
    build(nc, *args)
    r = _run(nc, [arrays], core_ids=[0])
    return r.results[0]["out_0"]
```

```python
from contextlib import ExitStack

import concourse.bass as bass
from concourse import mybir

F32 = mybir.dt.float32
F16 = mybir.dt.float16
BF16 = mybir.dt.bfloat16
I32 = mybir.dt.int32
U32 = mybir.dt.uint32
ALU = mybir.AluOpType
ACT = mybir.ActivationFunctionType
AX_X = mybir.AxisListType.X

P = 128
D = 128
E = 16
TOPK = 2
F = 176
FA = 128
FB = F - FA
UB = 64
NTOK = 8 * 1024
CAP = -(-5 * NTOK * TOPK // (4 * E))
NB = 8
TB = 8
BT = TB * P
CH = 256
CB = BT // CH
CE = CAP // CH
JE = CAP // P
NCH = E * CE
SW = D + 4
GW = 2 * FA + 112
BL = 32
WIN = P + 2 * BL
HW_ = WIN // 2
PADT = BT + 2 * BL
WS = 64.0
BIG = float(1 << 20)
MAGIC = 0x5F3759DF
EPS = 1e-5
ATT = float(1.0 / (D ** 0.5))
NX = 3
NXE = 3
ZW = 1024
RING = CE

K_ID, K_TRI, K_ONE, K_BLK = 0, 128, 256, 384
K_MASK = 512
K_IOTA = K_MASK + 3 * WIN
K_T2 = K_IOTA + E
K_POS = K_T2 + TB
K_N = K_POS + JE


ORDER_R = [("bs", 1, 2), ("si", 2, 2), ("yt", 0, 2), ("sc", 0, 2), ("hd", 2, 2), ("gu", 3, 2), ("ap", 0, 1),
           ("hi", 0, 1), ("dn", 1, 2), ("lo", 0, 1), ("yt", 1, 2), ("bs", 0, 1), ("si", 3, 2), ("t", 0, 1),
           ("dn", 2, 2), ("ap", 1, 1), ("hi", 1, 1), ("hd", 3, 2), ("xt", 0, 1), ("yt", 2, 2), ("sc", 1, 2),
           ("t", 1, 1), ("lo", 1, 1), ("xt", 1, 1), ("sc", 2, 2), ("t", 2, 1), ("sc", 3, 2), ("xt", 2, 1),
           ("t", 3, 1), ("xt", 3, 1), ("norm", 0, 0), ("lg", 0, 1), ("rt", 0, 1), ("gu", 0, 1), ("si", 0, 1),
           ("gu", 1, 1), ("pos", 0, 1), ("hd", 0, 1), ("gu", 2, 1), ("ex", 0, 1), ("pl", 0, 1), ("dn", 3, 2),
           ("yt", 3, 2), ("si", 1, 1), ("dn", 0, 1), ("hd", 1, 1)]
ORDER_M = [("dn", 3, 5), ("addb", 1, 2), ("ad", 0, 3), ("hi", 0, 3), ("v", 0, 2), ("yt", 3, 5), ("dn", 0, 4),
           ("ad", 1, 3), ("hd", 1, 4), ("yt", 0, 4), ("ys", 0, 0), ("s", 1, 2), ("vc", 0, 2), ("v", 1, 2),
           ("pt", 0, 2), ("hi", 1, 3), ("mx", 1, 2), ("pe", 1, 2), ("t", 0, 3), ("cad", 0, 1), ("s", 2, 2),
           ("xd", 0, 3), ("pta", 0, 2), ("pt", 1, 2), ("bs", 0, 3), ("t", 1, 3), ("iv", 0, 2), ("mx", 2, 2),
           ("v", 2, 2), ("o", 0, 2), ("vc", 1, 2), ("xt", 1, 3), ("pl_lo", 0, 3), ("t", 2, 3), ("chi", 0, 1),
           ("cad", 1, 1), ("pe", 2, 2), ("bs", 1, 3), ("pl_lo", 1, 3), ("x2", 0, 2), ("sc", 2, 4), ("comb", 0, 0),
           ("clo", 0, 1), ("xt", 2, 3), ("s", 3, 2), ("t", 3, 3), ("mx", 3, 2), ("pta", 1, 2), ("xt", 3, 3),
           ("o", 1, 2), ("chi", 1, 1), ("iv", 1, 2), ("vc", 2, 2), ("iv", 2, 2), ("lg", 0, 3), ("pt", 2, 2),
           ("pta", 2, 2), ("x2", 1, 2), ("rt", 0, 3), ("vc", 3, 2), ("v", 3, 2), ("o", 2, 2), ("gu", 2, 4),
           ("pe", 3, 2), ("ex", 0, 3), ("ct", 0, 1), ("pos", 0, 3), ("pt", 3, 2), ("sc", 3, 4), ("x2", 2, 2),
           ("si", 2, 4), ("gu", 3, 4), ("si", 3, 4), ("pl", 0, 3), ("hd", 2, 4), ("dn", 1, 4), ("cx", 0, 1),
           ("pta", 3, 2), ("hd", 3, 4), ("ct", 1, 1), ("cx", 1, 1), ("o", 3, 2), ("clo", 1, 1), ("ct", 2, 1),
           ("qk", 0, 1), ("iv", 3, 2), ("cx", 2, 1), ("ct", 3, 1), ("dn", 2, 4), ("comb", 1, 0), ("yt", 1, 4),
           ("qc", 0, 1), ("qk", 1, 1), ("cx", 3, 1), ("x2", 3, 2), ("s", 0, 1), ("qc", 1, 1), ("addb", 0, 1),
           ("gu", 0, 3), ("ys", 1, 0), ("si", 0, 3), ("gu", 1, 3), ("sc", 0, 3), ("norm2", 0, 0), ("si", 1, 3),
           ("mx", 0, 1), ("pe", 0, 1), ("yt", 2, 4), ("sc", 1, 3), ("hd", 0, 3)]
ORDER_E = [("prep", 0, 0), ("rows", 0, 4), ("et", 0, 3), ("exx", 0, 3), ("gu", 0, 4), ("si", 0, 4), ("hd", 0, 4),
           ("dn", 0, 5), ("eo", 0, 5), ("es", 0, 5)]
ORDER_F = [("ys", 0, 0), ("comb", 0, 0), ("ys", 1, 0), ("comb", 1, 0)]


class At:

    def __init__(self):
        self.n = {name: 0 for name in ("t", "gu", "dn", "qk", "v", "o", "lg", "pos")}
        self.experts = False
        self.unit = {}

    def even(self):
        gu = self.n["gu"]
        return gu - 1 + gu % 2 if gu else 0

    def odd(self):
        return self.n["gu"] - self.n["gu"] % 2

    def step(self, name, item, part):
        if name in ("t", "ct", "et"):
            self.n["t"] += 1
            self.unit[name, item, part] = self.n["t"]
        elif name in self.n:
            self.n[name] += 1


def wait(eng, sem, value):
    if value > 0:
        eng.wait_ge(sem, value)


def run_steps(order, at, fns, n, first):
    for s in range(n + max(lag for _, _, lag in order)):
        for name, part, lag in order:
            item = s - lag + first
            here = 0 <= s - lag < n
            if name in fns and (here or name == "norm2"):
                fns[name](item, part)
            if here:
                at.step(name, item, part)


class Chain:

    def __init__(self, eng, sem, per_item, item):
        self.eng, self.sem, self.base, self.n = eng, sem, per_item * item, 0
        self.per_item = per_item

    def add(self, ins):
        self.n += 1
        return ins.then_inc(self.sem, 1)

    def after(self, n=None):
        wait(self.eng, self.sem, self.base + (self.n if n is None else n))

    def end(self):
        assert self.n == self.per_item, (self.n, self.per_item)


def build(nc, x, wpack, bcols, brow, mlps, consts, out):
    ctx = ExitStack()

    def sb(name, shape, dt=F32):
        return ctx.enter_context(nc.sbuf_tensor(name, shape, dt))

    def ps(name, shape, dt=F32):
        return ctx.enter_context(nc.psum_tensor(name, shape, dt))

    def sem(name):
        return ctx.enter_context(nc.semaphore(name))

    def sems(name, n):
        return [sem(f"{name}{i}") for i in range(n)]

    with ctx:
        slots = nc.dram_tensor("slots", (E * CAP, SW), F32, kind="Internal").ap()
        yrows = [nc.dram_tensor(f"yrows{i}", (TOPK * NTOK, D), F32, kind="Internal").ap() for i in range(2)]

        cst = sb("cst", [P, K_N])
        zero = sb("zero", [P, ZW])
        idh = sb("idh", [P, P], F16)
        tri = sb("tri", [P, P], BF16)
        one = sb("one", [P, P], BF16)
        blk = sb("blk", [P, P], BF16)
        msk = sb("msk", [P, 3, WIN], BF16)
        bcol = sb("bcol", [P, 2])
        bqs = sb("bqs", [P, 1])
        brw = sb("brw", [P, D + E])
        wraw = sb("wraw", [P, 3 * D + E])
        whl = sb("whl", [P, 2, 3 * D + E], F16)
        gst = [sb(f"gst{i}", [P, GW]) for i in range(3)]
        ghl = [sb(f"ghl{i}", [P, 2, GW], F16) for i in range(3)]
        wdn = [sb(f"wdn{i}", [P, 2, D]) for i in range(3)]
        st = [sb(f"st{i}", [P, TB, 6]) for i in "rc"]
        mv = [sb(f"mv{i}", [P, TB, 2]) for i in "rc"]
        ve = [sb(f"ve{i}", [P, TB]) for i in "rc"]
        nt = [sb(f"nt{i}", [P, 2, TB]) for i in "rc"]
        rs = [sb(f"rs{i}", [P, 2, TB]) for i in "rc"]
        nmr = [sb(f"nmr{i}", [P, TB]) for i in "rc"]
        X = [sb(f"X{i}", [P, TB, D]) for i in range(NX)]
        base = [sb(f"base{i}", [P, BT]) for i in range(NB)]
        xnr = sb("xnr", [P, TB, D])
        stg = [sb(f"stg{i}", [P, TB, SW]) for i in range(2)]
        xtr = [sb(f"xtr{i}", [P, 2, BT], F16) for i in range(2)]
        lg = sb("lg", [P, TB, E + 1])
        m8 = sb("m8", [P, TB, 8])
        i8 = sb("i8", [P, TB, 8], U32)
        oh = sb("oh", [P, TB, 2, E])
        ohs = sb("ohs", [P, TB, E], BF16)
        dl = sb("dl", [P, TB, E + 1])
        ex = sb("ex", [P, TB, E + 1])
        zz = sb("zz", [P, 3, TB])
        pp = sb("pp", [P, TB, 2])
        prod = sb("prod", [P, TB, 2, E])
        pk = sb("pk", [P, TB, 2])
        ov = sb("ov", [P, TB, 2])
        s1 = sb("s1", [P, TB, 2])
        slot_i = [sb(f"slot_i{i}", [P, TB, 2], I32) for i in range(2)]
        mred = sb("mred", [P, E])
        maccb = sb("maccb", [P, E], BF16)
        cnt = sb("cnt", [P, E])
        sA = [sb(f"sA{i}", [P, CH]) for i in range(2)]
        sB = [sb(f"sB{i}", [P, CH]) for i in range(2)]
        hA = [sb(f"hA{i}", [P, CH]) for i in range(2)]
        hB = [sb(f"hB{i}", [P, CH]) for i in range(2)]
        xe = [sb(f"xe{i}", [P, JE, SW]) for i in range(NXE)]
        xte = [sb(f"xte{i}", [P, 2, CH], F16) for i in range(2)]
        yst = [sb(f"yst{i}", [P, 2, D]) for i in range(RING)]
        inval = sb("inval", [P, JE])
        half = sb("half", [P, 2, JE])
        wsel = [sb(f"wsel{i}", [P, JE]) for i in range(2)]
        t2k = sb("t2k", [P, JE])
        row_i = [sb(f"row_i{i}", [P, JE], I32) for i in range(2)]
        yin = [sb(f"yin{i}", [P, TB, 2, D]) for i in range(NY)]
        xnc = sb("xnc", [P, TB, D])
        hlc = sb("hlc", [P, 2, TB, D], F16)
        xtc = [sb(f"xtc{i}", [P, 2, PADT], F16) for i in range(2)]
        qT = [sb(f"qT{i}", [P, BT]) for i in range(2)]
        kT = [sb(f"kT{i}", [P, PADT]) for i in range(2)]
        nm = [sb(f"nm{i}", [P, 2]) for i in range(2)]
        pr = [sb(f"pr{i}", [P, 2, WIN]) for i in range(2)]
        rsum = [sb(f"rsum{i}", [P, 2]) for i in range(2)]
        rinv = [sb(f"rinv{i}", [P, 2]) for i in range(2)]
        pts = [sb(f"pts{i}", [HW_, 2, 2, P]) for i in range(2)]
        vs = [sb(f"vs{i}", [HW_, 2, 2, D]) for i in range(2)]

        psGU = [ps(f"psGU{i}", [P, 2, CH]) for i in range(2)]
        psR_ = [ps(f"psR{i}", [P, 512]) for i in range(2)]
        psT_ = ps("psT", [P, 1024], F16)
        psY_ = ps("psY", [P, 512])
        psS = ps("psS", [P, 512])
        psP = ps("psP", [P, 512])
        psR = [t[:, 0:CH] for t in psR_]
        psV = psR_[0][0:HW_, :].rearrange("p (b d) -> p b d", d=D)
        psO = psR_[1][:, 0:2 * D].rearrange("p (t d) -> p t d", t=2)
        psT = psT_[:, 0:2 * CH].rearrange("p (h c) -> p h c", h=2)
        psL = psY_[:, 0:TB * E]
        psPos = psY_[:, TB * E:2 * TB * E]
        psY = psY_[:, 2 * D:4 * D].rearrange("p (t d) -> p t d", t=2)
        psS2 = psS[:, 0:2 * WIN].rearrange("p (t c) -> p t c", t=2)
        psPT = psP[0:HW_, :].rearrange("p (t w q) -> p t w q", t=2, w=2)

        ld_c = sem("const_loaded")
        ld_w = sem("weights_loaded")
        zeroed = sem("zero_tile_ready")
        split0 = sem("fixed_weights_split")
        cst_ok = sem("constants_cast")
        padded = sem("windows_padded")
        sp_ch = sem("fixed_hi_done")
        fill_s = sems("slots_filled", JE)
        fill_y = sems("yrows_filled", 2)
        x_ld = sems("x_loaded", NX)
        x_dv = sem("x2_done")
        ln_ch = sems("ln_chain", 2)
        ln_ok = sems("ln_stats_done", 2)
        xn_ok = sems("xn_done", 2)
        hi_ok = sems("hi_done", 2)
        lo_ok = sems("lo_done", 2)
        bs_ok = sem("base_done")
        t_ok = sem("transposed")
        xt_ok = sem("xt_copied")
        lg_ok = sem("logits_done")
        rt_ch = sem("route_chain")
        ohs_ok = sem("onehot_done")
        dl_ok = sem("delta_done")
        ex_ok = sem("exp_done")
        pos_ok = sem("positions_done")
        rt2_ch = sem("position_chain")
        idx_ok = sem("slot_index_done")
        cnt_mm = sem("count_summed")
        cnt_ok = sem("count_copied")
        scat = sems("rows_scattered", 2)
        gu_ok = sem("gate_up_done")
        silu_ok = sem("silu_done")
        h_ok = sem("hidden_done")
        y_ok = sem("mlp_out_done")
        y_cp = sem("mlp_out_taken")
        xe_ld = sems("slots_loaded", NXE)
        xe_first = sem("first_slots_loaded")
        wg_ld = sems("gate_up_loaded", 2)
        wd_ld = sems("down_loaded", 2)
        wsp = sem("expert_split")
        esp_ch = sem("expert_hi_done")
        ri_ch = sem("row_chain")
        ysc = sems("results_scattered", RING)
        y_ld = sems("results_loaded", 2 * NY)
        ys_ok = sem("results_summed")
        x1_ok = sem("x1_done")
        xb_ok = sem("v_bias_added")
        qk_ok = sem("qk_done")
        qk_cp = sem("qk_copied")
        v_ok = sem("v_done")
        v_cp = sem("v_copied")
        s_ok = sem("scores_done")
        nm_ok = sem("negmax_done")
        p_ok = sem("probs_done")
        pt_ok = sem("probs_transposed")
        pt_cp = sem("probs_t_copied")
        o_ok = sem("attention_done")
        ri_ok = sem("inverse_sum_done")
        out_ok = sems("out_stored", NX)

        x_v = x.rearrange("b (j p) d -> b p j d", p=P)
        out_v = out.rearrange("b (j p) d -> b p j d", p=P)
        slots_v = slots.rearrange("(e p j) w -> e p (j w)", e=E, p=P)
        slots_e = slots.rearrange("(e c) w -> e c w", e=E)
        yr_v = [t.rearrange("(m j p k) d -> m p j (k d)", m=NB, j=TB, p=P) for t in yrows]

        def hi_of(rows):
            return rows[:, :, 0:D // 2].bitcast(F16)

        def lo_of(rows):
            return rows[:, :, D // 2:D].bitcast(F16)

        def tiles(h):
            return slice(h * TB // 2, (h + 1) * TB // 2)

        def chunk(g, i):
            return g * CB + i + (NCH if g >= NB else 0)

        def run_all(pieces):
            at = At()
            fns = pieces(at)
            for layer in range(2):
                if layer == 0:
                    run_steps(ORDER_R, at, fns, NB, 0)
                else:
                    run_steps(ORDER_M, at, fns, NB, NB)
                fns["counts"](layer)
                at.experts = True
                run_steps(ORDER_E, at, fns, NCH, NCH * layer)
                at.experts = False
            run_steps(ORDER_F, at, fns, NB, 2 * NB)

        block = ctx.enter_context(nc.Block())

        @block.sync
        def _(sp):
            def load_x(g):
                wait(sp, bs_ok, 2 * (g - NX + 1))
                sp.dma_start(X[g % NX][:], x_v[g]).then_inc(x_ld[g % NX], 16)

            def load_gate_up(e, layer):
                g = e + E * layer
                wait(sp, wsp, g - 1)
                sp.dma_start(gst[e % 2][:], mlps[e][:, 0:GW]).then_inc(wg_ld[e % 2], 16)

            def load_down(e, layer):
                g = e + E * layer
                wait(sp, y_ok, chunk_end(g - 2))
                sp.dma_start(wdn[e % 2][:].rearrange("p a d -> p (a d)"),
                             mlps[e][:, GW:]).then_inc(wd_ld[e % 2], 16)

            def chunk_end(g):
                return 0 if g < 0 else (g + 1) * CE + NB * CB * (g // E + 1)

            load_x(0)
            sp.dma_start(cst[:], consts).then_inc(ld_c, 16)
            sp.dma_start(wraw[:], wpack).then_inc(ld_w, 16)
            sp.dma_start(bcol[:], bcols).then_inc(ld_w, 16)
            sp.dma_start(brw[:], brow.broadcast_to([P, D + E])).then_inc(ld_w, 16)
            sp.dma_start(gst[2][:], mlps[E][:, 0:GW]).then_inc(ld_w, 16)
            sp.dma_start(wdn[2][:].rearrange("p a d -> p (a d)"), mlps[E][:, GW:]).then_inc(ld_w, 16)
            sp.wait_ge(zeroed, 1)

            def fill(dst, s):
                sp.dma_start(dst, zero[:, 0:dst.shape[2]].rearrange("p (o w) -> p o w", o=1)
                             .broadcast_to(list(dst.shape))).then_inc(s, 16)

            for j in range(JE):
                fill(slots_e[:, j * P:(j + 1) * P, :].rearrange("e p w -> p e w"), fill_s[j])
                if j < 2:
                    load_x(j + 1)

            load_gate_up(0, 0)
            load_down(0, 0)
            load_gate_up(1, 0)
            load_down(1, 0)
            load_x(3)
            load_x(4)
            def fill_rows(layer, i):
                rows = yrows[layer].rearrange("(p f a) w -> p f (a w)", p=P, f=N_FILL_Y * 4)
                fill(rows[:, 4 * i:4 * i + 4, :], fill_y[layer])

            for i in range(N_FILL_Y):
                fill_rows(0, i)
                if i + 5 < NB:
                    load_x(i + 5)

            def experts(layer):
                for k in range(2):
                    sp.wait_ge(scat[k], 16 * 2 * TB * (NB // 2) * (layer + 1))
                for e in range(E):
                    g = e + E * layer
                    if g >= NXE:
                        wait(sp, xt_ok, unit_end[g - NXE])
                        wait(sp, ri_ch, (g - NXE + 1) * N_RI)
                    rows, done = xe[g % NXE][:].rearrange("p j w -> p (j w)"), 0
                    if e == 0:
                        done = 2 * SW
                        sp.dma_start(rows[:, 0:done], slots_v[e][:, 0:done]).then_inc(xe_first, 16)
                    sp.dma_start(rows[:, done:], slots_v[e][:, done:]).then_inc(xe_ld[g % NXE], 16)
                    if 1 <= e < E - 1:
                        load_gate_up(e + 1, layer)
                        load_down(e + 1, layer)

            def results(m, phase):
                g = m + NB * phase
                wait(sp, x1_ok, 2 * (g - NY + 1))
                for h in range(2):
                    sp.dma_start(yin[g % NY][:, tiles(h)].rearrange("p j k d -> p j (k d)"),
                                 yr_v[phase][m][:, tiles(h), :]).then_inc(y_ld[2 * (g % NY) + h], 16)

            unit_end = [(e + 1) * CE + NB * CB + (2 * NB * CB if e >= E else 0) for e in range(2 * E)]

            experts(0)
            for i in range(RING):
                sp.wait_ge(ysc[i], 32 * E)
            for m in range(NB):
                results(m, 0)
                if m >= NB - N_FILL_Y:
                    fill_rows(1, m - NB + N_FILL_Y)
            for e in range(2):
                load_gate_up(e, 1)
                load_down(e, 1)
            experts(1)
            for i in range(RING):
                sp.wait_ge(ysc[i], 64 * E)
            for m in range(NY - 1):
                results(m, 1)
            for m in range(NB):
                if m + NY - 1 < NB:
                    results(m + NY - 1, 1)
                for h in range(2):
                    sp.wait_ge(x1_ok, 2 * (m + NB) + h + 1)
                    sp.dma_start(out_v[m][:, tiles(h), :], X[m % NX][:, tiles(h), :]).then_inc(out_ok[m % NX], 16)
            for k in range(NX):
                sp.wait_ge(out_ok[k], 32 * len(range(k, NB, NX)))

        @block.gpsimd
        def _(pool):
            nc.gpsimd.memset(zero[:], 0.0).then_inc(zeroed, 1)
            for k in range(2):
                nc.gpsimd.memset(xtc[k][:], 0.0)
                nc.gpsimd.memset(kT[k][:], 0.0).then_inc(padded, 1)

            def pieces(at):
                def scatter_rows(g, q):
                    if q == 0:
                        if g == 1:
                            for i in range(JE):
                                pool.wait_ge(fill_s[i], 16)
                        pool.wait_ge(idx_ok, g + 1)
                    for j in range(2 * q, 2 * q + 2):
                        if g == 0:
                            pool.wait_ge(fill_s[j], 16)
                        for c in range(2):
                            nc.gpsimd.indirect_dma_start(
                                out=slots,
                                out_offset=bass.IndirectOffsetOnAxis(ap=slot_i[g % 2][:, j, c:c + 1], axis=0),
                                in_=stg[g % 2][:, j, :], in_offset=None, bounds_check=E * CAP - 1,
                                oob_is_err=False).then_inc(scat[g % 2], 16)

                def scatter_results(c, _):
                    if c % CE == 0:
                        if c % NCH == 0:
                            pool.wait_ge(fill_y[c // NCH], 16 * N_FILL_Y)
                        pool.wait_ge(ri_ch, (c // CE + 1) * N_RI)
                    layer = c // NCH
                    pool.wait_ge(y_cp, c + 1 + NB * CB * (layer + 1))
                    for t in range(2):
                        j = 2 * (c % CE) + t
                        nc.gpsimd.indirect_dma_start(
                            out=yrows[layer],
                            out_offset=bass.IndirectOffsetOnAxis(ap=row_i[c // CE % 2][:, j:j + 1], axis=0),
                            in_=yst[c % RING][:, t, :], in_offset=None, bounds_check=TOPK * NTOK - 1,
                            oob_is_err=False).then_inc(ysc[c % RING], 16)

                def y_sum(g, h):
                    b = g - NB
                    pool.wait_ge(y_ld[2 * (b % NY) + h], (b // NY + 1) * 16)
                    y = yin[b % NY][:, tiles(h), :, :]
                    nc.gpsimd.tensor_tensor(y[:, :, 0, :], y[:, :, 0, :], y[:, :, 1, :], ALU.add).then_inc(ys_ok, 1)

                def c_lo(g, h):
                    pool.wait_ge(hi_ok[1], 2 * (g - NB) + h + 1)
                    nc.gpsimd.tensor_tensor(hlc[:, 1, tiles(h), :], xnc[:, tiles(h), :], hlc[:, 0, tiles(h), :],
                                            ALU.subtract).then_inc(lo_ok[1], 1)

                def r_lo(g, h):
                    pool.wait_ge(hi_ok[0], 2 * g + h + 1)
                    nc.gpsimd.tensor_tensor(lo_of(stg[g % 2][:, tiles(h), :]), xnr[:, tiles(h), :],
                                            hi_of(stg[g % 2][:, tiles(h), :]), ALU.subtract).then_inc(lo_ok[0], 1)

                def add_bias(g, h):
                    pool.wait_ge(hi_ok[1], 2 * (g - NB) + h + 1)
                    nc.gpsimd.tensor_tensor(
                        X[(g - NB) % NX][:, tiles(h), :], X[(g - NB) % NX][:, tiles(h), :],
                        brw[:, 0:D].rearrange("p (o d) -> p o d", o=1).broadcast_to([P, TB // 2, D]),
                        ALU.add).then_inc(xb_ok, 1)

                return dict(sc=scatter_rows, es=scatter_results, ys=y_sum, clo=c_lo, pl_lo=r_lo, addb=add_bias,
                            counts=lambda layer: None)

            run_all(pieces)

        @block.scalar
        def _(act):
            act.wait_ge(ld_c, 16)
            nc.scalar.copy(idh[:], cst[:, K_ID:K_ID + P]).then_inc(cst_ok, 1)
            nc.scalar.copy(tri[:], cst[:, K_TRI:K_TRI + P])
            nc.scalar.copy(one[:], cst[:, K_ONE:K_ONE + P])
            nc.scalar.copy(blk[:], cst[:, K_BLK:K_BLK + P])
            nc.scalar.copy(msk[:].rearrange("p a c -> p (a c)"), cst[:, K_MASK:K_MASK + 3 * WIN]).then_inc(cst_ok, 1)

            def pieces(at):
                def apply_norm(which, src, dst, h, n):
                    act.wait_ge(ln_ok[which], n + 1)
                    wait(act, lo_ok[which], 2 * n + h - 1)
                    for j in range(TB)[tiles(h)]:
                        nc.scalar.activation(dst[:, j, :], src[:, j, :], ACT.Identity, bias=nmr[which][:, j:j + 1],
                                             scale=rs[which][:, 0, j:j + 1]).then_inc(xn_ok[which], 1)

                def r_apply(g, h):
                    wait(act, bs_ok, 2 * g + h - 1)
                    apply_norm(0, X[g % NB % NX], xnr, h, g)

                def c_apply(g, h):
                    apply_norm(1, X[(g - NB) % NX], xnc, h, g - NB)

                def r_hi(g, h):
                    act.wait_ge(xn_ok[0], g * TB + (h + 1) * TB // 2)
                    wait(act, scat[g % 2], g // 2 * (16 * 2 * TB))
                    nc.scalar.copy(hi_of(stg[g % 2][:, tiles(h), :]), xnr[:, tiles(h), :]).then_inc(hi_ok[0], 1)

                def c_hi(g, h):
                    act.wait_ge(xn_ok[1], (g - NB) * TB + (h + 1) * TB // 2)
                    if g > NB:
                        act.wait_ge(t_ok, at.unit["ct", g - 1, 2 * h + 1])
                    nc.scalar.copy(hlc[:, 0, tiles(h), :], xnc[:, tiles(h), :]).then_inc(hi_ok[1], 1)

                def r_xt(g, i):
                    act.wait_ge(t_ok, at.unit["t", g, i])
                    if g >= 2:
                        act.wait_ge(gu_ok, chunk(g - 2, i) + 1)
                        act.wait_ge(lg_ok, g - 1)
                    nc.scalar.copy(xtr[g % 2][:, :, i * CH:(i + 1) * CH], psT).then_inc(xt_ok, 1)

                def r_exp(g, _):
                    act.wait_ge(dl_ok, g + 1)
                    nc.scalar.activation(ex[:], dl[:], ACT.Exp).then_inc(ex_ok, 1)

                def silu(g, _):
                    c = silus[0]
                    silus[0] += 1
                    act.wait_ge(gu_ok, c + 1)
                    wait(act, h_ok, c - 1)
                    nc.scalar.activation(sA[c % 2][:], psGU[c % 2][:, 0, :], ACT.Silu, scale=1.0 / WS)
                    nc.scalar.activation(sB[c % 2][UB:UB + FB, :], psR[c % 2][0:FB, :], ACT.Silu,
                                         scale=1.0 / WS).then_inc(silu_ok, 1)

                def e_xt(c, _):
                    act.wait_ge(t_ok, at.unit["et", c, 0])
                    act.wait_ge(gu_ok, c - 1 + NB * CB * (c // NCH + 1))
                    nc.scalar.copy(xte[c % 2][:], psT).then_inc(xt_ok, 1)

                def e_out(c, _):
                    act.wait_ge(y_ok, c + 1 + NB * CB * (c // NCH + 1))
                    wait(act, ysc[c % RING], c // RING * 32)
                    act.wait_ge(ri_ch, (c // CE + 1) * N_RI)
                    for t in range(2):
                        j = 2 * (c % CE) + t
                        last = nc.scalar.mul(yst[c % RING][:, t, :], psY[:, t, :], wsel[c // CE % 2][:, j:j + 1])
                    last.then_inc(y_cp, 1)

                def c_xt(g, i):
                    m = g - NB
                    act.wait_ge(padded, 2)
                    act.wait_ge(t_ok, at.unit["ct", g, i])
                    wait(act, v_ok, (m - 1) * 4)
                    nc.scalar.copy(xtc[m % 2][:, :, BL + i * CH:BL + (i + 1) * CH], psT).then_inc(xt_ok, 1)

                def qk_copy(g, h):
                    m = g - NB
                    if m == 0 and h == 0:
                        act.wait_ge(split0, 3)
                        act.wait_ge(padded, 2)
                    act.wait_ge(qk_ok, m * 2 + h + 1)
                    wait(act, s_ok, (m - 1) * 4)
                    nc.scalar.activation(qT[m % 2][:, h * 512:(h + 1) * 512],
                                         psGU[0][:].rearrange("p a c -> p (a c)"), ACT.Identity,
                                         bias=bqs[:, 0:1], scale=ATT / WS)
                    nc.scalar.activation(kT[m % 2][:, BL + h * 512:BL + (h + 1) * 512],
                                         psGU[1][:].rearrange("p a c -> p (a c)"), ACT.Identity,
                                         bias=bcol[:, 1:2], scale=1.0 / WS).then_inc(qk_cp, 1)

                def v_copy(g, i):
                    n = (g - NB) * 4 + i
                    act.wait_ge(v_ok, n + 1)
                    wait(act, o_ok, n - 1)
                    nc.scalar.activation(vs[i % 2][:].rearrange("p t w d -> p (t w d)"),
                                         psV.rearrange("p b d -> p (b d)"), ACT.Copy,
                                         scale=1.0 / WS).then_inc(v_cp, 1)

                def probs(g, i):
                    n = (g - NB) * 4 + i
                    act.wait_ge(nm_ok, n + 1)
                    wait(act, pt_ok, n - 1)
                    wait(act, ri_ok, n - 1)
                    for t in range(2):
                        nc.scalar.activation(pr[i % 2][:, t, :], psS2[:, t, :], ACT.Exp,
                                             bias=nm[i % 2][:, t:t + 1], scale=1.0,
                                             accum_out=rsum[i % 2][:, t:t + 1]).then_inc(p_ok, 1)

                def pt_copy(g, i):
                    n = (g - NB) * 4 + i
                    act.wait_ge(pt_ok, n + 1)
                    wait(act, o_ok, n - 1)
                    nc.scalar.copy(pts[i % 2][:], psPT).then_inc(pt_cp, 1)

                return dict(ap=r_apply, cap=c_apply, hi=r_hi, chi=c_hi, xt=r_xt, ex=r_exp, si=silu, exx=e_xt, eo=e_out,
                            cx=c_xt,
                            qc=qk_copy, vc=v_copy, pe=probs, pta=pt_copy, counts=lambda layer: None)

            silus = [0]
            run_all(pieces)

        @block.tensor
        def _(pe):
            def three(dst, w_hi, w_lo, x_hi, x_lo, weights_first=True):
                for n, (a, b) in enumerate(((w_hi, x_hi), (w_hi, x_lo), (w_lo, x_hi))):
                    if not weights_first:
                        a, b = b, a
                    last = nc.tensor.matmul(dst, a, b, start=n == 0, stop=n == 2)
                return last

            pe.wait_ge(cst_ok, 2)

            def pieces(at):
                n = at.n

                def transposes(hi, lo, t0):
                    wait(pe, xt_ok, n["t"])
                    for t in range(2):
                        nc.tensor.transpose(psT[:, 0, t * P:(t + 1) * P], hi[:, t0 + t, :], idh[:])
                        last = nc.tensor.transpose(psT[:, 1, t * P:(t + 1) * P], lo[:, t0 + t, :], idh[:])
                    last.then_inc(t_ok, 1)

                def y_free():
                    wait(pe, y_cp, n["dn"])
                    wait(pe, rt_ch, (n["lg"] - 1) * N_RT + 1)
                    wait(pe, rt2_ch, (n["pos"] - 1) * N_RT2 + 5)

                def r_t(g, i):
                    pe.wait_ge(lo_ok[0], 2 * g + i // 2 + 1)
                    transposes(hi_of(stg[g % 2][:, :, :]), lo_of(stg[g % 2][:, :, :]), 2 * i)

                def c_t(g, i):
                    pe.wait_ge(lo_ok[1], 2 * (g - NB) + i // 2 + 1)
                    transposes(hlc[:, 0], hlc[:, 1], 2 * i)

                def e_t(c, _):
                    e = c // CE
                    if c % NCH == 0:
                        pe.wait_ge(xe_first, (e // E + 1) * 16)
                    elif c % CE == 0 or c % NCH == 1:
                        pe.wait_ge(xe_ld[e % NXE], (e // NXE + 1) * 16)
                    rows = xe[e % NXE][:, :, :]
                    transposes(hi_of(rows), lo_of(rows), 2 * (c % CE))

                def r_logits(g, _):
                    pe.wait_ge(xt_ok, at.unit["t", g, CB - 1])
                    if g == 0:
                        pe.wait_ge(split0, 3)
                    y_free()
                    for j in range(TB):
                        cols = slice(j * P, (j + 1) * P)
                        last = three(psL[:, j * E:(j + 1) * E], whl[:, 0, 3 * D:], whl[:, 1, 3 * D:],
                                     xtr[g % 2][:, 0, cols], xtr[g % 2][:, 1, cols], weights_first=False)
                    last.then_inc(lg_ok, 1)

                def r_pos(g, _):
                    y_free()
                    pe.wait_ge(ohs_ok, g + 1)
                    first = g % NB == 0
                    m = ohs[:, :, :].rearrange("p j e -> p (j e)")
                    last = nc.tensor.matmul(psPos, tri[:], m, start=True, stop=False)
                    for j in range(TB - 1):
                        last = nc.tensor.matmul(
                            psPos[:, (j + 1) * E:].rearrange("p (j e) -> p j e", e=E), one[:],
                            ohs[:, j:j + 1, :].broadcast_to([P, TB - 1 - j, E]), start=False,
                            stop=first and j == TB - 2)
                    if not first:
                        pe.wait_ge(rt2_ch, g * N_RT2)
                        last = nc.tensor.matmul(psPos.rearrange("p (j e) -> p j e", e=E), one[:],
                                                maccb[:, :].rearrange("p (o e) -> p o e", o=1)
                                                .broadcast_to([P, TB, E]), start=False, stop=True)
                    last.then_inc(pos_ok, 1)

                def counts(layer):
                    pe.wait_ge(rt2_ch, NB * (layer + 1) * N_RT2)
                    y_free()
                    nc.tensor.matmul(psPos[:, 0:E], one[:], maccb[:], start=True, stop=True).then_inc(cnt_mm, 1)
                    pe.wait_ge(cnt_ok, layer + 1)

                def gate_up(item, i):
                    c = n["gu"]
                    if c == 0:
                        pe.wait_ge(split0, 3)
                    par = c % 2
                    if at.experts:
                        w, xt, cols = item // CE % 2, xte[item % 2], slice(0, CH)
                        if item % CE == 0:
                            pe.wait_ge(wsp, item // CE + 1)
                        pe.wait_ge(xt_ok, at.unit["et", item, 0])
                    else:
                        w, xt, cols = 2, xtr[item % 2], slice(i * CH, (i + 1) * CH)
                        pe.wait_ge(xt_ok, at.unit["t", item, i])
                    wait(pe, h_ok, c - 1)
                    wait(pe, qk_cp, n["qk"])
                    if par == 0:
                        wait(pe, v_cp, n["v"])
                    else:
                        wait(pe, x_dv, 2 * n["o"])
                    hl = ghl[w]
                    for a in range(2):
                        three(psGU[par][:, a, :], hl[:, 0, a * FA:(a + 1) * FA], hl[:, 1, a * FA:(a + 1) * FA],
                              xt[:, 0, cols], xt[:, 1, cols])
                    three(psR[par][0:GW - 2 * FA, :], hl[:, 0, 2 * FA:GW], hl[:, 1, 2 * FA:GW],
                          xt[:, 0, cols], xt[:, 1, cols]).then_inc(gu_ok, 1)

                def down(item, i):
                    c = n["dn"]
                    par = c % 2
                    w = item // CE % 2 if at.experts else 2
                    if at.experts and item % CE == 0:
                        pe.wait_ge(wd_ld[w], (item // CE // 2 + 1) * 16)
                    pe.wait_ge(h_ok, c + 1)
                    y_free()
                    for t in range(2):
                        cols = slice(t * P, (t + 1) * P)
                        nc.tensor.matmul(psY[:, t, :], hA[par][:, cols], wdn[w][:, 0, :], start=True, stop=False)
                        last = nc.tensor.matmul(psY[:, t, :], hB[par][:, cols], wdn[w][:, 1, :],
                                                start=False, stop=True)
                    last.then_inc(y_ok, 1)

                def qk(g, h):
                    m = g - NB
                    pe.wait_ge(xt_ok, at.unit["ct", g, 2 * h + 1])
                    wait(pe, qk_cp, n["qk"])
                    wait(pe, h_ok, n["gu"])
                    cols = slice(BL + h * 512, BL + (h + 1) * 512)
                    for a in range(2):
                        last = three(psGU[a][:].rearrange("p a c -> p (a c)"), whl[:, 0, a * D:(a + 1) * D],
                                     whl[:, 1, a * D:(a + 1) * D], xtc[m % 2][:, 0, cols], xtc[m % 2][:, 1, cols])
                    last.then_inc(qk_ok, 1)

                def scores(g, i):
                    m = g - NB
                    pe.wait_ge(qk_cp, m * 2 + (1 if i == 0 else 2))
                    wait(pe, p_ok, (m * 4 + i) * 2)
                    for t in range(2):
                        j = 2 * i + t
                        mk = 0 if j == 0 else 2 if j == TB - 1 else 1
                        nc.tensor.matmul(psS2[:, t, :], blk[:], msk[:, mk, :], start=True, stop=False)
                        last = nc.tensor.matmul(psS2[:, t, :], qT[m % 2][:, j * P:(j + 1) * P],
                                                kT[m % 2][:, j * P:j * P + WIN], start=False, stop=True)
                    last.then_inc(s_ok, 1)

                def values(g, i):
                    m = g - NB
                    wait(pe, v_cp, n["v"])
                    wait(pe, h_ok, at.even())
                    for t in range(2):
                        for w in range(2):
                            o = (2 * i + t) * P + w * HW_
                            last = three(psV[:, 2 * t + w, :],
                                         whl[:, 0, 2 * D:3 * D], whl[:, 1, 2 * D:3 * D],
                                         xtc[m % 2][:, 0, o:o + HW_], xtc[m % 2][:, 1, o:o + HW_],
                                         weights_first=False)
                    last.then_inc(v_ok, 1)

                def probs_t(g, i):
                    k = (g - NB) * 4 + i
                    pe.wait_ge(p_ok, k * 2 + 2)
                    wait(pe, pt_cp, k)
                    for t in range(2):
                        for w in range(2):
                            last = nc.tensor.transpose(psPT[:, t, w, :], pr[i % 2][:, t, w * HW_:(w + 1) * HW_],
                                                       cst[:, K_ID:K_ID + P])
                    last.then_inc(pt_ok, 1)

                def attend(g, i):
                    k = (g - NB) * 4 + i
                    pe.wait_ge(pt_cp, k + 1)
                    pe.wait_ge(v_cp, k + 1)
                    wait(pe, x_dv, 2 * n["o"])
                    wait(pe, h_ok, at.odd())
                    for t in range(2):
                        for w in range(2):
                            last = nc.tensor.matmul(psO[:, t, :], pts[i % 2][:, t, w, :], vs[i % 2][:, t, w, :],
                                                    start=w == 0, stop=w == 1)
                    last.then_inc(o_ok, 1)

                return dict(t=r_t, ct=c_t, et=e_t, lg=r_logits, pos=r_pos, gu=gate_up, dn=down, qk=qk, s=scores,
                            v=values, pt=probs_t, o=attend, counts=counts)

            run_all(pieces)

        @block.vector
        def _(dve):
            def split(dst, src, n):
                nc.vector.tensor_scalar(dst[:, 0], src, WS, None, ALU.mult).then_inc(sp_ch, 1)
                dve.wait_ge(sp_ch, n)
                nc.vector.scalar_tensor_tensor(out=dst[:, 1], in0=src, scalar=WS, in1=dst[:, 0],
                                               op0=ALU.mult, op1=ALU.subtract).then_inc(split0, 1)

            def prepare():
                for k in range(2):
                    nc.vector.memset(hB[k][:], 0.0)
                dve.wait_ge(ld_w, 16 * N_LDW)
                split(whl, wraw[:], 1)
                split(ghl[2], gst[2][:], 2)
                nc.vector.tensor_scalar(bqs[:], bcol[:, 0:1], ATT, None, ALU.mult).then_inc(split0, 1)

            def norm_steps(which, src, n):
                c = Chain(dve, ln_ch[which], N_LN, n)
                for j in range(TB):
                    c.add(nc.vector.bn_stats(st[which][:, j, :], src[:, j, :]))
                yield
                for j in range(TB):
                    c.after(j + 1)
                    c.add(nc.vector.bn_aggr(mv[which][:, j, :], st[which][:, j, :]))
                yield
                c.after()
                c.add(nc.vector.tensor_scalar(ve[which][:], mv[which][:, :, 1], EPS, None, ALU.add))
                yield
                c.after()
                a, b = nt[which][:, 0, :], nt[which][:, 1, :]
                y, y2 = rs[which][:, 0, :], rs[which][:, 1, :]
                v = ve[which][:]
                wait(dve, xn_ok[which], n * TB)
                c.add(nc.vector.tensor_scalar(y.bitcast(I32), v.bitcast(I32), -0.5, float(MAGIC),
                                              ALU.mult, ALU.add))
                for out, in0, scalar, in1, op0, op1 in (
                        (a, y, 1.0, y, ALU.mult, ALU.mult),
                        (b, a, 1.0, v, ALU.mult, ALU.mult),
                        (a, b, -10.0 / 3, b, ALU.add, ALU.mult),
                        (y2, a, 5.0, y, ALU.add, ALU.mult),
                        (a, y2, -0.5 * FACTOR ** 3, y2, ALU.mult, ALU.mult),
                        (b, a, 1.0, v, ALU.mult, ALU.mult),
                        (y, b, 1.5 * FACTOR, y2, ALU.add, ALU.mult)):
                    yield
                    c.after()
                    c.add(nc.vector.scalar_tensor_tensor(out=out, in0=in0, scalar=scalar, in1=in1, op0=op0,
                                                         op1=op1))
                yield
                c.after()
                nc.vector.scalar_tensor_tensor(out=nmr[which][:], in0=mv[which][:, :, 0], scalar=-1.0, in1=y,
                                               op0=ALU.mult, op1=ALU.mult).then_inc(ln_ok[which], 1)
                c.end()

            def pieces(at):
                n = at.n

                def norm(g, _):
                    dve.wait_ge(x_ld[g % NX], (g // NX + 1) * 16)
                    for _ in norm_steps(0, X[g % NX], g):
                        pass
                    if g == 0:
                        prepare()

                def norm2(g, _):
                    m, r = g - NB, g - 2
                    runs = []
                    if m < NB:
                        dve.wait_ge(x1_ok, 2 * (m + 1))
                        runs.append(norm_steps(1, X[m % NX], m))
                    if NB <= r < 2 * NB:
                        dve.wait_ge(x_dv, (r - NB + 1) * TB)
                        runs.append(norm_steps(0, X[r % NB % NX], r))
                    while runs:
                        for run in list(runs):
                            if next(run, 0) == 0:
                                runs.remove(run)

                def apply_norm(which, src, dst, h, n):
                    dve.wait_ge(ln_ok[which], n + 1)
                    wait(dve, lo_ok[which], 2 * n + h - 1)
                    for j in range(TB)[tiles(h)]:
                        nc.vector.tensor_scalar(dst[:, j, :], src[:, j, :], rs[which][:, 0, j:j + 1],
                                                nmr[which][:, j:j + 1], ALU.mult,
                                                ALU.add).then_inc(xn_ok[which], 1)

                def r_apply(g, h):
                    wait(dve, bs_ok, 2 * g + h - 1)
                    apply_norm(0, X[g % NB % NX], xnr, h, g)

                def c_apply(g, h):
                    apply_norm(1, X[(g - NB) % NX], xnc, h, g - NB)

                def r_lo(g, h):
                    dve.wait_ge(hi_ok[0], 2 * g + h + 1)
                    nc.vector.tensor_tensor(lo_of(stg[g % 2][:, tiles(h), :]), xnr[:, tiles(h), :],
                                            hi_of(stg[g % 2][:, tiles(h), :]), ALU.subtract).then_inc(lo_ok[0], 1)

                def r_base(g, h):
                    dve.wait_ge(hi_ok[0], 2 * g + h + 1)
                    if g >= NB:
                        dve.wait_ge(x1_ok, 2 * (g - NB + 1))
                    nc.vector.scalar_tensor_tensor(
                        out=base[g % NB][:, h * BT // 2:(h + 1) * BT // 2].rearrange("p (j d) -> p j d", d=D),
                        in0=xnr[:, tiles(h), :], scalar=0.5, in1=X[g % NB % NX][:, tiles(h), :], op0=ALU.mult,
                        op1=ALU.add).then_inc(bs_ok, 1)

                def r_route(g, _):
                    k = g % 2
                    c = Chain(dve, rt_ch, N_RT, g)
                    dve.wait_ge(lg_ok, g + 1)
                    c.add(nc.vector.scalar_tensor_tensor(
                        out=lg[:, :, 0:E], in0=psL.rearrange("p (j e) -> p j e", e=E), scalar=1.0 / WS,
                        in1=brw[:, D:].rearrange("p (o e) -> p o e", o=1).broadcast_to([P, TB, E]),
                        op0=ALU.mult, op1=ALU.add))
                    if g == 0:
                        dve.wait_ge(ld_c, 16)
                    c.after()
                    for j in range(TB):
                        c.add(nc.vector.max(m8[:, j, :], lg[:, j, 0:E]))
                    best = c.n
                    for j in range(TB):
                        c.after(best - TB + 1 + j)
                        c.add(nc.vector.max_index(i8[:, j, :], m8[:, j, :], lg[:, j, 0:E]))
                        if j == TB // 2:
                            c.after(best)
                            c.add(nc.vector.tensor_copy(lg[:, :, E:E + 1], m8[:, :, 1:2]))
                            beside = c.n
                    c.after(beside)
                    wait(dve, ex_ok, g)
                    nc.vector.tensor_tensor(dl[:], lg[:], m8[:, :, 0:1].broadcast_to([P, TB, E + 1]),
                                            ALU.subtract).then_inc(dl_ok, 1)
                    indexed = c.n
                    c.add(nc.vector.tensor_scalar(stg[k][:, :, D:D + 1].rearrange("p j o -> p (j o)"),
                                                  cst[:, K_T2:K_T2 + TB], float(2 * BT * (g % NB)), None, ALU.add))
                    c.after(indexed)
                    c.add(nc.vector.tensor_tensor(
                        oh[:], i8[:, :, 0:2].rearrange("p j (k o) -> p j k o", o=1).broadcast_to([P, TB, 2, E]),
                        cst[:, K_IOTA:K_IOTA + E].rearrange("p (a b e) -> p a b e", a=1, b=1)
                        .broadcast_to([P, TB, 2, E]), ALU.is_equal))
                    shown = c.n
                    c.add(nc.vector.tensor_copy(stg[k][:, :, D + 1:D + 2], i8[:, :, 0:1]))
                    c.after(shown)
                    wait(dve, pos_ok, g)
                    nc.vector.tensor_tensor(ohs[:], oh[:, :, 0, :], oh[:, :, 1, :], ALU.add).then_inc(ohs_ok, 1)
                    c.end()

                def r_place(g, _):
                    k = g % 2
                    c = Chain(dve, rt2_ch, N_RT2, g)
                    dve.wait_ge(ex_ok, g + 1)
                    dve.wait_ge(ohs_ok, g + 1)
                    z, s, q = zz[:, 0, :], zz[:, 1, :], zz[:, 2, :]
                    c.add(nc.vector.tensor_reduce(z, ex[:, :, 0:E], AX_X, ALU.add))
                    c.add(nc.vector.tensor_reduce(mred[:], ohs[:, :, :].rearrange("p j e -> p e j"), AX_X,
                                                  ALU.add))
                    c.after(1)
                    c.add(nc.vector.reciprocal(pp[:, :, 0], z))
                    c.after(3)
                    c.add(nc.vector.tensor_tensor(pp[:, :, 1], ex[:, :, E], pp[:, :, 0], ALU.mult))
                    dve.wait_ge(pos_ok, g + 1)
                    c.add(nc.vector.tensor_tensor(
                        prod[:], oh[:], psPos.rearrange("p (j o e) -> p j o e", o=1, e=E)
                        .broadcast_to([P, TB, 2, E]), ALU.mult))
                    c.after(4)
                    c.add(nc.vector.scalar_tensor_tensor(out=s, in0=pp[:, :, 0], scalar=1e-9, in1=pp[:, :, 1],
                                                         op0=ALU.add, op1=ALU.add))
                    c.after(5)
                    c.add(nc.vector.tensor_reduce(pk[:], prod[:], AX_X, ALU.add))
                    c.after(6)
                    c.add(nc.vector.reciprocal(q, s))
                    if g % NB == 0:
                        c.add(nc.vector.tensor_copy(maccb[:], mred[:]))
                    else:
                        c.add(nc.vector.tensor_tensor(maccb[:], maccb[:], mred[:], ALU.add))
                    c.after(7)
                    c.add(nc.vector.tensor_scalar(ov[:], pk[:], float(CAP), BIG, ALU.is_ge, ALU.mult))
                    c.add(nc.vector.scalar_tensor_tensor(out=s1[:], in0=i8[:, :, 0:2], scalar=float(CAP), in1=pk[:],
                                                         op0=ALU.mult, op1=ALU.add))
                    c.after(8)
                    c.add(nc.vector.tensor_tensor(
                        stg[k][:, :, D + 2:D + 4], pp[:], zz[:, 2, :].rearrange("p (j o) -> p j o", o=1)
                        .broadcast_to([P, TB, 2]), ALU.mult))
                    c.after(11)
                    wait(dve, scat[k], g // 2 * (16 * 2 * TB))
                    nc.vector.tensor_tensor(slot_i[k][:], s1[:], ov[:], ALU.add).then_inc(idx_ok, 1)
                    c.end()

                def hidden(item, _):
                    c = hids[0]
                    hids[0] += 1
                    par = c % 2
                    dve.wait_ge(silu_ok, c + 1)
                    wait(dve, y_ok, c - 1)
                    nc.vector.scalar_tensor_tensor(out=hA[par][:], in0=psGU[par][:, 1, :], scalar=1.0 / WS,
                                                   in1=sA[par][:], op0=ALU.mult, op1=ALU.mult)
                    nc.vector.scalar_tensor_tensor(out=hB[par][UB:UB + FB, :], in0=psR[par][UB:UB + FB, :],
                                                   scalar=1.0 / WS, in1=sB[par][UB:UB + FB, :], op0=ALU.mult,
                                                   op1=ALU.mult).then_inc(h_ok, 1)

                def take(g, i):
                    dve.wait_ge(y_ok, chunk(g, i) + 1)
                    dve.wait_ge(bs_ok, 2 * g + i // 2 + 1)
                    b = base[g % NB][:, i * CH:(i + 1) * CH]
                    nc.vector.scalar_tensor_tensor(
                        out=b, in0=psY.rearrange("p t d -> p (t d)"), scalar=0.5, in1=b,
                        op0=ALU.mult, op1=ALU.add).then_inc(y_cp, 1)

                def counts(layer):
                    dve.wait_ge(cnt_mm, layer + 1)
                    nc.vector.tensor_copy(cnt[:], psPos[:, 0:E]).then_inc(cnt_ok, 1)
                    dve.wait_ge(cnt_ok, layer + 1)

                def e_prep(item, _):
                    if item % CE:
                        return
                    g = item // CE
                    par = g % 2
                    dve.wait_ge(wg_ld[par], (g // 2 + 1) * 16)
                    wait(dve, gu_ok, (g - 1) * CE + NB * CB * ((g - 2) // E + 1) if g > 1 else 0)
                    nc.vector.tensor_scalar(ghl[par][:, 0], gst[par][:], WS, None, ALU.mult).then_inc(esp_ch, 1)
                    dve.wait_ge(esp_ch, g + 1)
                    nc.vector.scalar_tensor_tensor(out=ghl[par][:, 1], in0=gst[par][:], scalar=WS,
                                                   in1=ghl[par][:, 0], op0=ALU.mult,
                                                   op1=ALU.subtract).then_inc(wsp, 1)

                def e_rows(item, _):
                    if item % CE:
                        return
                    g = item // CE
                    e, par = g % E, g % 2
                    dve.wait_ge(xe_ld[g % NXE], (g // NXE + 1) * 16)
                    dve.wait_ge(xe_first, (g // E + 1) * 16)
                    wait(dve, ri_ch, g * N_RI)
                    nc.vector.tensor_scalar(inval[:], cst[:, K_POS:K_POS + JE], cnt[:, e:e + 1], BIG,
                                            ALU.is_ge, ALU.mult).then_inc(ri_ch, 1)
                    words = xe[g % NXE][:, :, D:SW].rearrange("p j w -> p w j")
                    first = words[:, 1, :]
                    column = cst[:, K_IOTA + e:K_IOTA + e + 1]
                    nc.vector.scalar_tensor_tensor(out=t2k[:], in0=first, scalar=column, in1=words[:, 0, :],
                                                   op0=ALU.not_equal, op1=ALU.add).then_inc(ri_ch, 1)
                    nc.vector.tensor_scalar(half[:, 0], first, column, 0.5, ALU.is_equal, ALU.mult)
                    nc.vector.tensor_scalar(half[:, 1], first, column, 0.5, ALU.not_equal, ALU.mult).then_inc(ri_ch, 1)
                    dve.wait_ge(ri_ch, g * N_RI + 2)
                    for i in range(RING):
                        wait(dve, ysc[i], (g - 1) * 32)
                    nc.vector.tensor_tensor(row_i[par][:], inval[:], t2k[:], ALU.add).then_inc(ri_ch, 1)
                    dve.wait_ge(ri_ch, g * N_RI + 3)
                    nc.vector.tensor_tensor(half[:], half[:], words[:, 2:4, :], ALU.mult).then_inc(ri_ch, 1)
                    dve.wait_ge(ri_ch, g * N_RI + 5)
                    wait(dve, y_cp, (g - 1) * CE + NB * CB * ((g - 2) // E + 1) if g > 1 else 0)
                    nc.vector.tensor_tensor(wsel[par][:], half[:, 0], half[:, 1], ALU.add).then_inc(ri_ch, 1)

                def combine(g, h):
                    b = g - NB
                    m = b % NB
                    dve.wait_ge(y_cp, chunk(b, 2 * h + 1) + 1)
                    dve.wait_ge(ys_ok, 2 * b + h + 1)
                    dve.wait_ge(bs_ok, 4 * NB if b >= NB else 2 * (NB + max(m - NX + 1, 0)))
                    if b >= NB:
                        wait(dve, out_ok[m % NX], m // NX * 32)
                    nc.vector.tensor_tensor(
                        X[m % NX][:, tiles(h), :],
                        base[m][:, h * BT // 2:(h + 1) * BT // 2].rearrange("p (j d) -> p j d", d=D),
                        yin[b % NY][:, tiles(h), 0, :], ALU.add).then_inc(x1_ok, 1)

                def neg_max(g, i):
                    k = (g - NB) * 4 + i
                    dve.wait_ge(s_ok, k + 1)
                    wait(dve, p_ok, (k - 1) * 2)
                    nc.vector.tensor_reduce(nm[i % 2][:], psS2, AX_X, ALU.max, negate=True).then_inc(nm_ok, 1)

                def pt_copy(g, i):
                    k = (g - NB) * 4 + i
                    dve.wait_ge(pt_ok, k + 1)
                    wait(dve, o_ok, k - 1)
                    nc.vector.tensor_copy(pts[i % 2][:], psPT).then_inc(pt_cp, 1)

                def v_copy(g, i):
                    k = (g - NB) * 4 + i
                    dve.wait_ge(v_ok, k + 1)
                    wait(dve, o_ok, k - 1)
                    nc.vector.tensor_scalar(vs[i % 2][:].rearrange("p t w d -> p (t w d)"),
                                            psV.rearrange("p b d -> p (b d)"), 1.0 / WS, None,
                                            ALU.mult).then_inc(v_cp, 1)

                def r_xt(g, i):
                    dve.wait_ge(t_ok, at.unit["t", g, i])
                    if g >= 2:
                        dve.wait_ge(gu_ok, chunk(g - 2, i) + 1)
                        dve.wait_ge(lg_ok, g - 1)
                    nc.vector.tensor_copy(xtr[g % 2][:, :, i * CH:(i + 1) * CH], psT).then_inc(xt_ok, 1)

                def c_xt(g, i):
                    m = g - NB
                    dve.wait_ge(padded, 2)
                    dve.wait_ge(t_ok, at.unit["ct", g, i])
                    wait(dve, v_ok, (m - 1) * 4)
                    nc.vector.tensor_copy(xtc[m % 2][:, :, BL + i * CH:BL + (i + 1) * CH], psT).then_inc(xt_ok, 1)

                def c_lo(g, h):
                    dve.wait_ge(hi_ok[1], 2 * (g - NB) + h + 1)
                    nc.vector.tensor_tensor(hlc[:, 1, tiles(h), :], xnc[:, tiles(h), :], hlc[:, 0, tiles(h), :],
                                            ALU.subtract).then_inc(lo_ok[1], 1)

                def inverse(g, i):
                    k = (g - NB) * 4 + i
                    dve.wait_ge(p_ok, k * 2 + 2)
                    wait(dve, x_dv, 2 * (k - 1))
                    nc.vector.reciprocal(rinv[i % 2][:], rsum[i % 2][:]).then_inc(ri_ok, 1)

                def x2(g, i):
                    m = g - NB
                    k = m * 4 + i
                    dve.wait_ge(ri_ok, k + 1)
                    dve.wait_ge(xb_ok, 2 * m + i // 2 + 1)
                    dve.wait_ge(o_ok, k + 1)
                    for t in range(2):
                        rows = X[m % NX][:, 2 * i + t, :]
                        nc.vector.scalar_tensor_tensor(out=rows, in0=psO[:, t, :], scalar=rinv[i % 2][:, t:t + 1],
                                                       in1=rows, op0=ALU.mult, op1=ALU.add).then_inc(x_dv, 1)

                return dict(norm=norm, norm2=norm2, lo=r_lo, bs=r_base, rt=r_route, pl=r_place, hd=hidden, yt=take,
                            counts=counts, prep=e_prep, rows=e_rows, comb=combine, mx=neg_max, ptc=pt_copy,
                            iv=inverse, x2=x2, ad=r_apply, cad=c_apply, vd=v_copy, xd=r_xt, cd=c_xt, cl=c_lo)

            hids = [0]
            run_all(pieces)


FACTOR = 0.375
N_LN = 2 * TB + 9
N_RT = 1 + 2 * TB + 2 + 2
N_RT2 = 12
N_RI = 6
N_LDW = 5
N_FILL_Y = 4
NY = 3


def constants():
    import numpy as np
    c = np.zeros((P, K_N), np.float32)
    i = np.arange(P)
    c[:, K_ID:K_ID + P] = np.eye(P)
    c[:, K_TRI:K_TRI + P] = i[:, None] < i[None, :]
    c[:, K_ONE:K_ONE + P] = 1
    for b in range(P // BL):
        c[b, K_BLK + BL * b:K_BLK + BL * (b + 1)] = 1
        for v in range(3):
            m = c[b, K_MASK + v * WIN:K_MASK + (v + 1) * WIN]
            m[:] = -1e30
            m[BL * b:BL * (b + 3)] = 0
            if v == 0:
                m[:BL] = -1e30
            if v == 2:
                m[WIN - BL:] = -1e30
    c[:, K_IOTA:K_IOTA + E] = np.arange(E)
    c[:, K_T2:K_T2 + TB] = 2 * (np.arange(TB)[None] * P + i[:, None])
    c[:, K_POS:K_POS + JE] = i[:, None] * JE + np.arange(JE)[None]
    return c


_INS = ['L0_attn_x', 'L0_attn_Wq', 'L0_attn_bq', 'L0_attn_Wk', 'L0_attn_bk', 'L0_attn_Wv', 'L0_attn_bv',
        'L0_ffn_router_w', 'L0_ffn_router_b', 'L0_ffn_w_gate', 'L0_ffn_w_up', 'L0_ffn_w_down',
        'L0_ffn_sw_gate', 'L0_ffn_sw_up', 'L0_ffn_sw_down']


def layout(inputs):
    import numpy as np
    (x, wq, bq, wk, bk, wv, bv, rw, rb, wg, wu, wd, sg, su, sd) = [np.asarray(inputs[name]) for name in _INS]
    mlps = np.zeros((E + 1, P, GW + 2 * D), np.float32)
    for i in range(E + 1):
        g, u, d = (wg[i], wu[i], wd[i]) if i < E else (sg, su, sd)
        mlps[i, :, 0:FA] = g[:, 0:FA]
        mlps[i, :, FA:2 * FA] = u[:, 0:FA]
        mlps[i, :, 2 * FA:2 * FA + FB] = g[:, FA:]
        mlps[i, :, 2 * FA + UB:2 * FA + UB + FB] = u[:, FA:]
        mlps[i, :, GW:GW + D] = d[0:FA]
        mlps[i, UB:UB + FB, GW + D:] = d[FA:]
    return {"x": np.ascontiguousarray(x),
            "qkv_router": np.concatenate([wq, wk, wv, rw], axis=1),
            "qk_bias": np.stack([bq, bk], axis=1),
            "v_router_bias": np.concatenate([bv, rb])[None],
            "mlps": mlps,
            "constants": constants()}


def kernel(**inputs):
    import concourse.bacc as _bacc
    from concourse.bass_utils import run_bass_kernel_spmd as _run

    nc = _bacc.Bacc("TRN2", target_bir_lowering=False, num_devices=1)
    arrays = layout(inputs)
    args = [nc.dram_tensor(name, a.shape, mybir.dt.from_np(a.dtype), kind="ExternalInput").ap()
            for name, a in arrays.items()]
    args.append(nc.dram_tensor("out_0", (NB, BT, D), F32, kind="ExternalOutput").ap())
    build(nc, *args)
    r = _run(nc, [arrays], core_ids=[0])
    return r.results[0]["out_0"]
```
